# Optimizing a Trainium2 kernel written in Bass

```python
import numpy as np
import jax
import jax.numpy as jnp

def _softmax(x, axis=-1):
    return jax.nn.softmax(x, axis=axis)

def _gelu(x):
    return jax.nn.gelu(x, approximate=True)

def _silu(x):
    return jax.nn.silu(x)

def _sigmoid(x):
    return jax.nn.sigmoid(x)

def _layernorm(x, axis=-1, eps=1e-05):
    m = jnp.mean(x, axis=axis, keepdims=True)
    v = jnp.var(x, axis=axis, keepdims=True)
    return (x - m) / jnp.sqrt(v + eps)

def _scatter_add(tgt, idx, src, axis=0):
    return tgt.at[idx].add(src)

def _segment_sum(src, seg, n):
    return jax.ops.segment_sum(src, seg, n)
kernel_name = 'mk_seq_preln_d1_jaxref_r8_c5e590'

def setup_inputs(seed: int=0):
    np.random.seed(seed)
    _w = jnp.asarray

    def _L0_attn_setup():
        import jax, jax.numpy as jnp
        import numpy as np
        MIN_TIMESCALE = 1.0
        MAX_TIMESCALE = 10000.0

        def llama_rope(x):
            B, S, N, H = x.shape
            half = H // 2
            fraction = 2.0 * jnp.arange(0, half, dtype=jnp.float32) / H
            timescale = MIN_TIMESCALE * (MAX_TIMESCALE / MIN_TIMESCALE) ** fraction
            position = jnp.arange(S, dtype=jnp.float32)[None, :, None, None]
            sinusoid = position / timescale[None, None, None, :]
            sin, cos = (jnp.sin(sinusoid), jnp.cos(sinusoid))
            xr = x.astype(jnp.float32).reshape(B, S, N, half, 2)
            x1, x2 = (xr[..., 0], xr[..., 1])
            r1 = x1 * cos - x2 * sin
            r2 = x2 * cos + x1 * sin
            out = jnp.stack((r1, r2), axis=-1).reshape(B, S, N, H)
            return out.astype(x.dtype)
        key = jax.random.key(seed)
        kx, kq, kk, kv, ko = jax.random.split(key, 5)
        B, S, D, N, H = (4, 256, 256, 16, 128)
        x = jax.random.normal(kx, (B, S, D), dtype=jnp.float32)
        wq = jax.random.normal(kq, (D, N, H), dtype=jnp.float32) / np.sqrt(D)
        wk = jax.random.normal(kk, (D, N, H), dtype=jnp.float32) / np.sqrt(D)
        wv = jax.random.normal(kv, (D, N, H), dtype=jnp.float32) / np.sqrt(D)
        wo = jax.random.normal(ko, (N, H, D), dtype=jnp.float32) / np.sqrt(N * H)
        return {'x': x, 'wq': wq, 'wk': wk, 'wv': wv, 'wo': wo}
    _L0_attn_in = _L0_attn_setup()

    def _L0_ffn_setup():
        import jax, jax.numpy as jnp
        import numpy as np
        B, S, H = (2, 256, 256)
        E, I, K = (8, 176, 2)
        SHARED_I = 176 * 2

        def _moe_forward(hidden_states, gate_w, w1, w3, w2, sw1, sw3, sw2):
            x = hidden_states.reshape(-1, H)
            T = x.shape[0]
            logits = x @ gate_w.T
            scores = jax.nn.softmax(logits, axis=-1)
            topk_w, topk_idx = jax.lax.top_k(scores, K)
            topk_w = topk_w / jnp.sum(topk_w, axis=-1, keepdims=True)
            h = jnp.einsum('th,ehi->eti', x, w1)
            g = jnp.einsum('th,ehi->eti', x, w3)
            y_all = jnp.einsum('eti,eih->eth', jax.nn.silu(h) * g, w2)
            tok = jnp.arange(T)[:, None]
            y_sel = y_all[topk_idx, tok]
            y = jnp.sum(y_sel * topk_w[..., None], axis=1)
            shared = jax.nn.silu(x @ sw1) * (x @ sw3) @ sw2
            return (y + shared).reshape(hidden_states.shape)
        key = jax.random.key(seed)
        ks = jax.random.split(key, 8)
        s = 0.02
        return {'hidden_states': jax.random.normal(ks[0], (B, S, H), jnp.float32), 'gate_w': jax.random.normal(ks[1], (E, H), jnp.float32) * s, 'w1': jax.random.normal(ks[2], (E, H, I), jnp.float32) * s, 'w3': jax.random.normal(ks[3], (E, H, I), jnp.float32) * s, 'w2': jax.random.normal(ks[4], (E, I, H), jnp.float32) * s, 'sw1': jax.random.normal(ks[5], (H, SHARED_I), jnp.float32) * s, 'sw3': jax.random.normal(ks[6], (H, SHARED_I), jnp.float32) * s, 'sw2': jax.random.normal(ks[7], (SHARED_I, H), jnp.float32) * s}
    _L0_ffn_in = _L0_ffn_setup()
    _d = {'L0_attn_x': _L0_attn_in['x'], 'L0_attn_wq': _L0_attn_in['wq'], 'L0_attn_wk': _L0_attn_in['wk'], 'L0_attn_wv': _L0_attn_in['wv'], 'L0_attn_wo': _L0_attn_in['wo'], 'L0_ffn_gate_w': _L0_ffn_in['gate_w'], 'L0_ffn_w1': _L0_ffn_in['w1'], 'L0_ffn_w3': _L0_ffn_in['w3'], 'L0_ffn_w2': _L0_ffn_in['w2'], 'L0_ffn_sw1': _L0_ffn_in['sw1'], 'L0_ffn_sw3': _L0_ffn_in['sw3'], 'L0_ffn_sw2': _L0_ffn_in['sw2']}
    _x0 = _d['L0_attn_x']
    _d['L0_attn_x'] = jax.random.normal(jax.random.fold_in(jax.random.key(seed), 1), (8, 256, 256), dtype=_x0.dtype)
    del _x0
    return _d

def reference(L0_attn_x, L0_attn_wq, L0_attn_wk, L0_attn_wv, L0_attn_wo, L0_ffn_gate_w, L0_ffn_w1, L0_ffn_w3, L0_ffn_w2, L0_ffn_sw1, L0_ffn_sw3, L0_ffn_sw2):

    def _L0_attn_ref(x, wq, wk, wv, wo):
        import jax, jax.numpy as jnp
        import numpy as np
        MIN_TIMESCALE = 1.0
        MAX_TIMESCALE = 10000.0

        def llama_rope(x):
            B, S, N, H = x.shape
            half = H // 2
            fraction = 2.0 * jnp.arange(0, half, dtype=jnp.float32) / H
            timescale = MIN_TIMESCALE * (MAX_TIMESCALE / MIN_TIMESCALE) ** fraction
            position = jnp.arange(S, dtype=jnp.float32)[None, :, None, None]
            sinusoid = position / timescale[None, None, None, :]
            sin, cos = (jnp.sin(sinusoid), jnp.cos(sinusoid))
            xr = x.astype(jnp.float32).reshape(B, S, N, half, 2)
            x1, x2 = (xr[..., 0], xr[..., 1])
            r1 = x1 * cos - x2 * sin
            r2 = x2 * cos + x1 * sin
            out = jnp.stack((r1, r2), axis=-1).reshape(B, S, N, H)
            return out.astype(x.dtype)
        q = jnp.einsum('bsd,dnh->bsnh', x, wq)
        k = jnp.einsum('bsd,dnh->bsnh', x, wk)
        v = jnp.einsum('bsd,dnh->bsnh', x, wv)
        q = llama_rope(q)
        k = llama_rope(k)
        head_dim = q.shape[-1]
        q = q / jnp.sqrt(jnp.asarray(head_dim, q.dtype))
        S = q.shape[1]
        logits = jnp.einsum('bqnh,bknh->bnqk', q, k)
        causal = jnp.tril(jnp.ones((S, S), dtype=bool))
        logits = jnp.where(causal[None, None, :, :], logits, jnp.asarray(-1e+30, logits.dtype))
        probs = jax.nn.softmax(logits.astype(jnp.float32), axis=-1).astype(v.dtype)
        attn = jnp.einsum('bnqk,bknh->bqnh', probs, v)
        return jnp.einsum('bqnh,nhd->bqd', attn, wo)

    def _L0_ffn_ref(hidden_states, gate_w, w1, w3, w2, sw1, sw3, sw2):
        import jax, jax.numpy as jnp
        import numpy as np
        B, S, H = (2, 256, 256)
        E, I, K = (8, 176, 2)
        SHARED_I = 176 * 2

        def _moe_forward(hidden_states, gate_w, w1, w3, w2, sw1, sw3, sw2):
            x = hidden_states.reshape(-1, H)
            T = x.shape[0]
            logits = x @ gate_w.T
            scores = jax.nn.softmax(logits, axis=-1)
            topk_w, topk_idx = jax.lax.top_k(scores, K)
            topk_w = topk_w / jnp.sum(topk_w, axis=-1, keepdims=True)
            h = jnp.einsum('th,ehi->eti', x, w1)
            g = jnp.einsum('th,ehi->eti', x, w3)
            y_all = jnp.einsum('eti,eih->eth', jax.nn.silu(h) * g, w2)
            tok = jnp.arange(T)[:, None]
            y_sel = y_all[topk_idx, tok]
            y = jnp.sum(y_sel * topk_w[..., None], axis=1)
            shared = jax.nn.silu(x @ sw1) * (x @ sw3) @ sw2
            return (y + shared).reshape(hidden_states.shape)
        return _moe_forward(hidden_states, gate_w, w1, w3, w2, sw1, sw3, sw2)
    x = L0_attn_x
    x = x + _L0_attn_ref(_layernorm(x, axis=-1), L0_attn_wq, L0_attn_wk, L0_attn_wv, L0_attn_wo)
    x = x + _L0_ffn_ref(_layernorm(x, axis=-1), L0_ffn_gate_w, L0_ffn_w1, L0_ffn_w3, L0_ffn_w2, L0_ffn_sw1, L0_ffn_sw3, L0_ffn_sw2)
    return x

_drawn_inputs = setup_inputs


def setup_inputs(seed=0):
    import zlib

    import numpy as np

    out = dict(_drawn_inputs(seed))
    spreads = {}
    factors = {'L0_ffn_gate_w': 6.691,
     'L0_ffn_w1': 5.867,
     'L0_ffn_w3': 5.818,
     'L0_ffn_w2': 5.807,
     'L0_ffn_sw1': 2.949,
     'L0_ffn_sw3': 2.915,
     'L0_ffn_sw2': 2.91}
    for name, (base, spread) in spreads.items():
        noise = np.random.default_rng([zlib.crc32(name.encode()), seed]).standard_normal(out[name].shape)
        drawn = base * np.exp(spread * noise) if base else spread * noise
        out[name] = jnp.asarray(drawn.astype(out[name].dtype))
    for name, factor in factors.items():
        out[name] = (out[name] * factor).astype(out[name].dtype)
    return out
```

```python
from contextlib import ExitStack

import numpy as np

import concourse.bass as bass
from concourse import mybir

F32 = mybir.dt.float32
F32R = mybir.dt.float32r
ALU = mybir.AluOpType
ACT = mybir.ActivationFunctionType
AX = mybir.AxisListType

P = 128
B, S, D = 8, 256, 256
N, H = 16, 128
DC = D // P
ST = S // P
G, GH = 4, 4
GW = GH * H
NT = B * ST
E, I = 8, 176
SI = 2 * I
UW = 2 * I
AW = SI + E * I
NB = -(-AW // P)
TAIL = AW - (NB - 1) * P
EPS = 1e-5
MASKED = -1e30
SCALE = float(H) ** -0.5
BIG = 3.0e38
NSTAGE = 4
CH = 1024


def attention_phase(nc, x, wq, wk, wv, wo, cos_t, sin_t, mask_t, ident_t, resid):
    ctx = ExitStack()
    with ctx:
        def sb(name, shape, dt=F32):
            return ctx.enter_context(nc.sbuf_tensor(name, shape, dt))

        def ps(name, shape):
            return ctx.enter_context(nc.psum_tensor(name, shape, F32))

        def sem(name):
            return ctx.enter_context(nc.semaphore(name))

        wqk = [[sb(f"w{a}_{b}", [P, G, DC, GH, H], F32R) for b in ("hi", "lo")] for a in "qk"]
        wvs = [sb(f"wv_{b}", [P, G, DC, GW], F32R) for b in ("hi", "lo")]
        wos = [sb(f"wo_{b}", [P, N, D], F32R) for b in ("hi", "lo")]
        cosn = sb("cosn", [P, S])
        sinn = sb("sinn", [P, S])
        mask = sb("mask", [P, S])
        ident = sb("ident", [P, P])
        xn = sb("xn", [P, ST, D])
        xnt = [sb(f"xnt_{b}", [P, DC, S], F32R) for b in ("hi", "lo")]
        work = sb("work", [P, NSTAGE * CH])
        rope_cos = work[:, 0:2 * 512].rearrange("p (a c s) -> p a c s", a=2, c=2)
        rope_sin = work[:, 1024:2048].rearrange("p (a c s) -> p a c s", a=2, c=2)
        roped = work[:, 2048:3072].rearrange("p (a c s) -> p a c s", a=2, c=2)
        negs = [work[:, 3072 + 384 * a:3456 + 384 * a] for a in range(2)]
        prob = [sb(f"prob{a}", [P, 3 * P]) for a in range(2)]
        qkt = [[sb(f"qkt_{b}{a}", [P, 2, S], F32R) for b in ("hi", "lo")] for a in range(2)]
        vs = [[sb(f"v_{b}{a}", [P, ST, GW], F32R) for b in ("hi", "lo")] for a in range(2)]
        pts = [sb(f"pt_{b}", [P, 4, P], F32R) for b in ("hi", "lo")]
        att = [[sb(f"att_{b}{a}", [P, S], F32R) for b in ("hi", "lo")] for a in range(2)]
        stats = sb("stats", [P, ST, 6])
        mv = sb("mv", [P, ST, 2])
        vare = sb("vare", [P, ST])
        rstd = sb("rstd", [P, ST])
        mhalf = sb("mhalf", [P, ST])
        bias = sb("bias", [P, 2, ST])
        rsum = sb("rsum", [P, 2, ST])
        rinv = sb("rinv", [P, 2, ST])

        p_qk = [ps(f"p_qk{a}", [P, 2, S]) for a in range(2)]
        p_v = ps("p_v", [P, GW])
        p_s = [ps(f"p_s{a}", [P, ST, S]) for a in range(2)]
        p_t = ps("p_t", [P, 4, P])
        p_o = ps("p_o", [P, 2, S])
        p_y = ps("p_y", [P, ST, D])

        x_in = sem("x_in")
        tables_in = sem("tables_in")
        staged = [sem(f"staged{a}") for a in range(NSTAGE)]
        w_hi = sem("w_hi")
        w_lo = sem("w_lo")
        consts = sem("consts")
        stats_done = sem("stats_done")
        mv_done = sem("mv_done")
        vare_done = sem("vare_done")
        rstd_done = sem("rstd_done")
        xn_done = sem("xn_done")
        xnt_ps = sem("xnt_ps")
        xnt_hi = sem("xnt_hi")
        xnt_lo = sem("xnt_lo")
        resid_done = sem("resid_done")
        v_ps = sem("v_ps")
        v_hi = sem("v_hi")
        v_lo = sem("v_lo")
        qk_ps = sem("qk_ps")
        rope_mul = sem("rope_mul")
        rope_add = sem("rope_add")
        qkt_hi = sem("qkt_hi")
        qkt_lo = sem("qkt_lo")
        s_ps = sem("s_ps")
        max0 = sem("max0")
        max1 = sem("max1")
        exp0 = sem("exp0")
        exp1 = sem("exp1")
        inv_done = sem("inv_done")
        prob_done = sem("prob_done")
        pt_ps = sem("pt_ps")
        pt_hi = sem("pt_hi")
        pt_lo = sem("pt_lo")
        o_ps = sem("o_ps")
        o_hi = sem("o_hi")
        o_lo = sem("o_lo")
        y_ps = sem("y_ps")

        pieces = []
        for g in range(G):
            for m, w in enumerate((wq, wk)):
                src = w.rearrange("(c p) n h -> p c (n h)", p=P)[:, :, g * GW:(g + 1) * GW]
                pieces.append((src, wqk[m][0][:, g], wqk[m][1][:, g], True))
            src = wv.rearrange("(c p) n h -> p c (n h)", p=P)[:, :, g * GW:(g + 1) * GW]
            pieces.append((src, wvs[0][:, g], wvs[1][:, g], False))
        for g in range(G):
            src = wo.rearrange("n h d -> h n d")[:, g * GH:(g + 1) * GH, :]
            pieces.append((src, wos[0][:, g * GH:(g + 1) * GH], wos[1][:, g * GH:(g + 1) * GH], False))

        def piece_views(n):
            _, hi, lo, permuted = pieces[n]
            raw = work[:, (n % NSTAGE) * CH:(n % NSTAGE + 1) * CH]
            if permuted:
                view = "p c n (two j) -> p (c n) two j"
                return (raw.rearrange("p (m j two) -> p m two j", two=2, j=H // 2),
                        hi.rearrange(view, two=2), lo.rearrange(view, two=2))
            flat = "p a b -> p (a b)"
            return raw, hi.rearrange(flat), lo.rearrange(flat)

        block = ctx.enter_context(nc.Block())

        @block.sync
        def _(sp):
            x_t = x.rearrange("b (t p) d -> p (b t) d", p=P)
            sp.dma_start(resid[:, 0:ST, :], x_t[:, 0:ST, :]).then_inc(x_in, 16)
            for dst, src in ((ident, ident_t), (cosn, cos_t), (sinn, sin_t), (mask, mask_t)):
                sp.dma_start(dst[:, :], src).then_inc(tables_in, 16)
            for n, (src, _, _, _) in enumerate(pieces):
                if n >= NSTAGE:
                    sp.wait_ge(w_lo, n - NSTAGE + 1)
                dst = work[:, (n % NSTAGE) * CH:(n % NSTAGE + 1) * CH]
                a = src.shape[1]
                sp.dma_start(dst.rearrange("p (a b) -> p a b", a=a), src).then_inc(staged[n % NSTAGE], 16)
                if n == 6:
                    sp.dma_start(resid[:, ST:NT, :], x_t[:, ST:NT, :]).then_inc(x_in, 16)

        @block.tensor
        def _(pe):
            def three(out, lhs, rhs, start, stop, more=False):
                for n, (a, b) in enumerate(((1, 0), (0, 1), (0, 0))):
                    mm = pe.matmul(out, lhs[a], rhs[b], start=start and n == 0, stop=stop and n == 2,
                                   skip_group_check=more)
                return mm

            def transpose_xn(c0):
                pe.wait_ge(xn_done, c0 + 1)
                for c in range(DC):
                    for t in range(ST):
                        mm = pe.transpose(p_v[:, c * S + t * P:c * S + (t + 1) * P],
                                          xn[:, t, c * P:(c + 1) * P], ident[:, :])
                mm.then_inc(xnt_ps, 1)

            def project(j, h):
                g, n = h // GH, h % GH
                for m in range(2):
                    for c in range(DC):
                        w = [wqk[m][b][:, g, c, n] for b in range(2)]
                        mm = three(p_qk[h % 2][:, m, :], w, [xnt[b][:, c] for b in range(2)],
                                   c == 0, c == DC - 1)
                mm.then_inc(qk_ps, 1)

            def values(g, t):
                for c in range(DC):
                    mm = three(p_v[:, :], [xnt[b][:, c, t * P:(t + 1) * P] for b in range(2)],
                               [wvs[b][:, g, c] for b in range(2)], c == 0, c == DC - 1)
                mm.then_inc(v_ps, 1)

            def scores(h):
                a = h % 2
                for t in range(ST):
                    mm = three(p_s[a][:, t, :], [qkt[a][b][:, 0, t * P:(t + 1) * P] for b in range(2)],
                               [qkt[a][b][:, 1, :] for b in range(2)], True, True)
                mm.then_inc(s_ps, 1)

            def transpose_probs(h):
                a = h % 2
                for slot, src in ((2, 0), (3, P), (1, 2 * P)):
                    mm = pe.transpose(p_t[:, slot, :], prob[a][:, src:src + P], ident[:, :])
                mm.then_inc(pt_ps, 1)

            def attend(h):
                g, n = h // GH, h % GH
                for k in range(ST):
                    v = [vs[g % 2][b][:, k, n * H:(n + 1) * H] for b in range(2)]
                    pt = [pts[b][:, 2 * (1 - k):2 * (1 - k) + 2, :] for b in range(2)]
                    mm = three(p_o[:, h % 2, :], v, pt, k == 0, k == ST - 1)
                mm.then_inc(o_ps, 1)

            def output(h):
                a = h % 2
                for t in range(ST):
                    mm = three(p_y[:, t, :], [att[a][b][:, t * P:(t + 1) * P] for b in range(2)],
                               [wos[b][:, h, :] for b in range(2)], h == 0 and t == 0,
                               h == N - 1 and t == ST - 1, more=True)
                mm.then_inc(y_ps, 1)

            pe.wait_ge(tables_in, 64)
            transpose_xn(0)
            pe.wait_ge(w_lo, 3)
            pe.wait_ge(xnt_lo, 1)
            for h in range(3):
                if h == 2:
                    pe.wait_ge(rope_mul, 1)
                project(h, h)
                if h < 2:
                    if h:
                        pe.wait_ge(v_lo, h)
                    values(0, h)
            pe.wait_ge(qkt_lo, 1)
            scores(0)
            pe.wait_ge(w_lo, len(pieces))
            pe.wait_ge(consts, 2)

            with pe.Fori(0, B) as b:
                j0 = b * N
                for h in range(N):
                    pe.wait_ge(prob_done, j0 + h + 1)
                    transpose_probs(h)
                    pe.wait_ge(qkt_lo, j0 + h + 2)
                    scores((h + 1) % N)
                    last = h == N - 1
                    if h == 12:
                        pe.wait_ge(v_lo, b * 8 + 8)
                        transpose_xn(b + 1)
                    if h == 13:
                        pe.wait_ge(xnt_lo, b + 2)
                    project(None, (h + 3) % N)
                    if h % 2 == 1 and not last:
                        unit = 2 + h // 2
                        pe.wait_ge(v_lo, b * 8 + unit)
                        values((h // GH + 1) % G, (h // 2) % 2)
                    pe.wait_ge(pt_lo, j0 + h + 1)
                    if h % GH == 0:
                        pe.wait_ge(v_lo, b * 8 + 2 * (h // GH) + 2)
                    attend(h)
                    if last:
                        pe.wait_ge(v_lo, b * 8 + 9)
                        values(0, 1)
                    if h >= 1:
                        pe.wait_ge(o_lo, j0 + h)
                        if h == 1:
                            pe.wait_ge(resid_done, b + 1)
                        output(h - 1)
                    if last:
                        pe.wait_ge(o_lo, j0 + N)
                        output(h)

        @block.vector
        def _(dve):
            def norm_stats(first):
                for t in range(ST):
                    src = resid[:, first + t, :]
                    op = nc.vector.bn_stats(stats[:, t, :], src)
                op.then_inc(stats_done, 1)

            def norm_mv(c0):
                dve.wait_ge(stats_done, c0 + 1)
                dve.nop(nofuse=True)
                for t in range(ST):
                    op = nc.vector.bn_aggr(mv[:, t, :], stats[:, t, :])
                op.then_inc(mv_done, 1)

            def norm_x(c0, first):
                dve.wait_ge(rstd_done, c0 + 1)
                for t in range(ST):
                    op = nc.vector.tensor_scalar(xn[:, t, :], resid[:, first + t, :], mv[:, t, 0:1],
                                                 rstd[:, t:t + 1], ALU.subtract, ALU.mult)
                op.then_inc(xn_done, 1)

            def rope_cosines(h):
                a = h % 2
                c = cosn[:, None, :].to_broadcast([P, 2, S])
                nc.vector.tensor_tensor(rope_cos[:, a], p_qk[a][:, :, :], c, ALU.mult)

            def rope_sines(h):
                a = h % 2
                for lo, hi in ((0, 64), (64, 0)):
                    sn = sinn[lo:lo + 64, None, :].to_broadcast([64, 2, S])
                    op = nc.vector.tensor_tensor(rope_sin[lo:lo + 64, a], p_qk[a][hi:hi + 64, :, :], sn,
                                                 ALU.mult)
                op.then_inc(rope_mul, 1)

            def mask_and_max(h, t):
                a = h % 2
                if t == 0:
                    nc.vector.tensor_tensor_reduce(negs[a][:, 0:P], p_s[a][:, 0, 0:P], mask[:, P:2 * P], -SCALE, BIG,
                                                   ALU.add, ALU.min, bias[:, a, 0:1]).then_inc(max0, 1)
                else:
                    nc.vector.tensor_tensor_reduce(negs[a][:, P:3 * P], p_s[a][:, 1, :], mask[:, :], -SCALE, BIG,
                                                   ALU.add, ALU.min, bias[:, a, 1:2]).then_inc(max1, 1)

            def invert(h):
                nc.vector.reciprocal(rinv[:, h % 2, :], rsum[:, h % 2, :]).then_inc(inv_done, 1)

            def value_lo(u):
                a = (u // 2) % 2
                nc.vector.tensor_tensor(vs[a][1][:, u % 2, :], p_v[:, :], vs[a][0][:, u % 2, :],
                                        ALU.subtract).then_inc(v_lo, 1)

            def probs_lo():
                nc.vector.tensor_tensor(pts[1][:, 1:4, :], p_t[:, 1:4, :], pts[0][:, 1:4, :],
                                        ALU.subtract).then_inc(pt_lo, 1)

            def att_lo(h):
                a = h % 2
                nc.vector.tensor_tensor(att[a][1][:, :], p_o[:, a, :], att[a][0][:, :],
                                        ALU.subtract).then_inc(o_lo, 1)

            def xnt_low():
                nc.vector.tensor_tensor(xnt[1][:, :, :], p_v[:, :].rearrange("p (c s) -> p c s", c=DC),
                                        xnt[0][:, :, :], ALU.subtract).then_inc(xnt_lo, 1)

            nc.vector.memset(mhalf[:, :], -0.5).then_inc(resid_done, 1)
            nc.vector.memset(pts[0][:, 0, :].bitcast(F32), 0.0)
            nc.vector.memset(pts[1][:, 0, :].bitcast(F32), 0.0).then_inc(consts, 2)
            dve.wait_ge(x_in, 16)
            norm_stats(0)
            norm_mv(0)
            norm_x(0, 0)
            dve.wait_ge(xnt_hi, 1)
            xnt_low()
            for n in range(len(pieces)):
                raw, hi, lo = piece_views(n)
                dve.wait_ge(w_hi, n + 1)
                nc.vector.tensor_tensor(lo, raw, hi, ALU.subtract).then_inc(w_lo, 1)
            dve.wait_ge(w_lo, len(pieces))
            for h in range(3):
                dve.wait_ge(qk_ps, h + 1)
                if h == 2:
                    dve.wait_ge(rope_add, 1)
                rope_cosines(h)
                rope_sines(h)
                if h < 2:
                    dve.wait_ge(v_hi, h + 1)
                    value_lo(h)
            dve.wait_ge(s_ps, 1)
            mask_and_max(0, 0)
            mask_and_max(0, 1)
            dve.wait_ge(exp1, 1)
            invert(0)
            dve.wait_ge(x_in, 32)

            with dve.Fori(0, B) as b:
                j0 = b * N
                nxt = ((b + 1) % B) * ST
                for h in range(N):
                    last = h == N - 1
                    dve.wait_ge(pt_hi, j0 + h + 1)
                    probs_lo()
                    dve.wait_ge(s_ps, j0 + h + 2)
                    dve.nop(nofuse=True)
                    mask_and_max((h + 1) % N, 0)
                    mask_and_max((h + 1) % N, 1)
                    if h == 12:
                        dve.wait_ge(xnt_hi, b + 2)
                        xnt_low()
                    dve.wait_ge(qk_ps, j0 + h + 4)
                    dve.wait_ge(rope_add, j0 + h + 2)
                    rope_cosines((h + 3) % N)
                    dve.wait_ge(exp1, j0 + h + 2)
                    invert((h + 1) % N)
                    rope_sines((h + 3) % N)
                    if h % 2 == 1 and not last:
                        unit = (2 + h // 2) % 8
                        dve.wait_ge(v_hi, b * 8 + 3 + h // 2)
                        value_lo(unit)
                    dve.wait_ge(o_hi, j0 + h + 1)
                    att_lo(h)
                    if last:
                        dve.wait_ge(v_hi, b * 8 + 10)
                        value_lo(1)
                    if h == 6:
                        norm_stats(nxt)
                    if h == 7:
                        norm_mv(b + 1)
                    if h == 9:
                        norm_x(b + 1, nxt)
                dve.wait_ge(y_ps, j0 + N)
                nc.vector.tensor_tensor(resid[:, bass.ds(b * ST, ST), :], resid[:, bass.ds(b * ST, ST), :],
                                        p_y[:, :, :], ALU.add).then_inc(resid_done, 1)

        @block.scalar
        def _(act):
            def values_hi(u):
                a = (u // 2) % 2
                nc.scalar.copy(vs[a][0][:, u % 2, :], p_v[:, :]).then_inc(v_hi, 1)

            def qkt_high(h):
                a = h % 2
                nc.scalar.copy(qkt[a][0][:, :, :], roped[:, a]).then_inc(qkt_hi, 1)

            def exps(h, t):
                a = h % 2
                c = slice(0, P) if t == 0 else slice(P, 3 * P)
                nc.scalar.activation(prob[a][:, c], negs[a][:, c], ACT.Exp, bias=bias[:, a, t:t + 1], scale=-1.0,
                                     accum_out=rsum[:, a, t:t + 1]).then_inc((exp0, exp1)[t], 1)

            def normalise(h):
                a = h % 2
                nc.scalar.activation(prob[a][:, 0:P], prob[a][:, 0:P], ACT.Copy, scale=rinv[:, a, 0:1])
                nc.scalar.activation(prob[a][:, P:3 * P], prob[a][:, P:3 * P], ACT.Copy,
                                     scale=rinv[:, a, 1:2]).then_inc(prob_done, 1)

            def xnt_high():
                nc.scalar.copy(xnt[0][:, :, :], p_v[:, :].rearrange("p (c s) -> p c s", c=DC)).then_inc(xnt_hi, 1)

            act.wait_ge(xnt_ps, 1)
            xnt_high()
            for n in range(len(pieces)):
                raw, hi, lo = piece_views(n)
                act.wait_ge(staged[n % NSTAGE], 16 * (n // NSTAGE + 1))
                nc.scalar.copy(hi, raw).then_inc(w_hi, 1)
            for h in range(2):
                act.wait_ge(v_ps, h + 1)
                values_hi(h)
                act.wait_ge(rope_add, h + 1)
                qkt_high(h)
            for t in range(ST):
                act.wait_ge((max0, max1)[t], 1)
                exps(0, t)
            act.wait_ge(inv_done, 1)
            normalise(0)

            with act.Fori(0, B) as b:
                j0 = b * N
                for h in range(N):
                    last = h == N - 1
                    act.wait_ge(pt_ps, j0 + h + 1)
                    nc.scalar.copy(pts[0][:, 1:4, :], p_t[:, 1:4, :]).then_inc(pt_hi, 1)
                    for t in range(ST):
                        act.wait_ge((max0, max1)[t], j0 + h + 2)
                        exps((h + 1) % N, t)
                    if h == 12:
                        act.wait_ge(xnt_ps, b + 2)
                        act.wait_ge(qk_ps, j0 + N)
                        xnt_high()
                    act.wait_ge(rope_add, j0 + h + 3)
                    qkt_high((h + 2) % N)
                    act.wait_ge(inv_done, j0 + h + 2)
                    normalise((h + 1) % N)
                    if h % 2 == 1 and not last:
                        act.wait_ge(v_ps, b * 8 + 3 + h // 2)
                        values_hi((2 + h // 2) % 8)
                    act.wait_ge(o_ps, j0 + h + 1)
                    nc.scalar.copy(att[h % 2][0][:, :], p_o[:, h % 2, :]).then_inc(o_hi, 1)
                    if last:
                        act.wait_ge(v_ps, b * 8 + 10)
                        values_hi(1)

        @block.gpsimd
        def _(pool):
            def rsqrt(c0):
                pool.wait_ge(mv_done, c0 + 1)
                pool.nop(nofuse=True)
                nc.gpsimd.tensor_scalar(vare[:, :], mv[:, :, 1], EPS, 1.0, ALU.add, ALU.mult).then_inc(vare_done, 1)
                pool.wait_ge(vare_done, c0 + 1)
                nc.gpsimd.tensor_tensor(rstd[:, :], vare[:, :], mhalf[:, :], ALU.pow).then_inc(rstd_done, 1)

            def add(h):
                a = h % 2
                nc.gpsimd.tensor_tensor(roped[:, a], rope_cos[:, a], rope_sin[:, a], ALU.add).then_inc(rope_add, 1)

            def low(h):
                a = h % 2
                nc.gpsimd.tensor_tensor(qkt[a][1][:, :, :], roped[:, a], qkt[a][0][:, :, :],
                                        ALU.subtract).then_inc(qkt_lo, 1)

            rsqrt(0)
            for h in range(2):
                pool.wait_ge(rope_mul, h + 1)
                add(h)
                pool.wait_ge(qkt_hi, h + 1)
                low(h)

            with pool.Fori(0, B) as b:
                j0 = b * N
                for h in range(N):
                    pool.wait_ge(rope_mul, j0 + h + 3)
                    pool.wait_ge(qkt_lo, j0 + h + 1)
                    add((h + 2) % N)
                    pool.wait_ge(qkt_hi, j0 + h + 3)
                    low((h + 2) % N)
                    if h == 7:
                        rsqrt(b + 1)


def experts_phase(nc, gate_w, w1, w3, w2, sw1, sw3, sw2, ident_t, before_t, resid, out):
    ctx = ExitStack()
    with ctx:
        def sb(name, shape, dt=F32):
            return ctx.enter_context(nc.sbuf_tensor(name, shape, dt))

        def ps(name, shape):
            return ctx.enter_context(nc.psum_tensor(name, shape, F32))

        def sem(name):
            return ctx.enter_context(nc.semaphore(name))

        NU = E + 2
        UP = UW + E
        NR = E + 1
        ups = [sb(f"up_{b}", [P, NU, DC, UP], F32R) for b in ("hi", "lo")]
        downs = [sb(f"down_{b}", [P, NB, D], F32R) for b in ("hi", "lo")]
        stage = sb("stage", [P, NU, DC, UP])
        stage_d = sb("stage_d", [P, NB, D])
        ident = sb("ident2", [P, P])
        before = sb("before", [P, E, E])
        xn = sb("xn2", [P, D])
        xnt = [sb(f"xn2t_{b}", [P, DC, P], F32R) for b in ("hi", "lo")]
        silu = sb("silu", [P, 3, SI])
        acts = sb("acts", [P, NB * P])
        actt = [[sb(f"actt_{b}{a}", [P, 4, P], F32R) for b in ("hi", "lo")] for a in range(2)]
        stats = sb("stats2", [P, 6])
        mv = sb("mv2", [P, 2])
        vare = sb("vare2", [P, 1])
        rstd = sb("rstd2", [P, 1])
        mhalf = sb("mhalf2", [P, 1])
        logit = sb("logit", [P, E])
        top = sb("top", [P, 8])
        gap = sb("gap", [P, 1])
        th = sb("th", [P, 1])
        wtop = sb("wtop", [P, 2])
        above = sb("above", [P, E, E])
        equal = sb("equal", [P, E, E])
        rank = sb("rank", [P, E])
        wfirst = sb("wfirst", [P, E])
        wt = sb("wt", [P, E])

        p_u = [ps(f"p_u{a}", [P, 512]) for a in range(4)]
        p_x = ps("p_x", [P, DC, P])
        p_a = [ps(f"p_a{a}", [P, 4, P]) for a in range(2)]
        p_y = ps("p_y2", [P, D])

        consts_in = sem("consts_in")
        staged = [sem(f"staged_up{u}") for u in range(NU)]
        staged_d = sem("staged_d")
        w_hi = sem("w_hi2")
        w_lo = sem("w_lo2")
        stats_done = sem("stats2_done")
        mv_done = sem("mv2_done")
        vare_done = sem("vare2_done")
        rstd_done = sem("rstd2_done")
        xn_done = sem("xn2_done")
        xnt_ps = sem("xn2t_ps")
        xnt_hi = sem("xn2t_hi")
        xnt_lo = sem("xn2t_lo")
        gap_done = sem("gap_done")
        th_done = sem("th_done")
        router = sem("router")
        y_ps = sem("y2_ps")
        res_done = sem("res_done")
        stored = sem("stored")
        u_ps = sem("u_ps")
        silu_done = sem("silu_done")
        act_done = sem("act_done")
        a_ps = sem("a_ps")
        a_hi = sem("a_hi")
        a_lo = sem("a_lo")

        groups = [list(range(g, min(g + 4, NB))) for g in range(0, NB, 4)]
        NG = len(groups)
        rows = [P] * (NB - 1) + [TAIL]
        ready = [2 + max(0, -(-(min(g[-1] * P + P, AW) - SI - I) // I)) for g in groups]
        RS = 8

        def read_by(u):
            return (1, 2, 2)[u] if u < 3 else u

        def spans(g):
            n = len(groups[g])
            return [(0, n, P)] if g < NG - 1 or TAIL == P else [(0, n - 1, P), (n - 1, n, TAIL)]

        block = ctx.enter_context(nc.Block())

        @block.sync
        def _(sp):
            def up_src(w):
                return w.rearrange("(c p) i -> p c i", p=P)

            sp.dma_start(ident[:, :], ident_t).then_inc(consts_in, 16)
            sp.dma_start(before[:, :, :], before_t).then_inc(consts_in, 16)
            for u in range(NU):
                if u in (1, 2):
                    sp.dma_start(stage[:, u, :, 0:UW], up_src((sw1, sw3)[u - 1])).then_inc(staged[u], 32)
                else:
                    e = max(0, u - 2)
                    sp.dma_start(stage[:, u, :, 0:I], up_src(w1[e])).then_inc(staged[u], 16)
                    sp.dma_start(stage[:, u, :, I:UW], up_src(w3[e])).then_inc(staged[u], 16)
                if u == 0:
                    with nc.allow_non_contiguous_dma(reason="the router's 2048 weights, transposed"):
                        for c in range(DC):
                            sp.dma_start(stage[:, 0, c, UW:UP],
                                         gate_w[:, c * P:(c + 1) * P].rearrange("e p -> p e"))\
                              .then_inc(staged[0], 16)
            down_parts = 0
            for src, first, count in [(sw2, 0, SI)] + [(w2[e], SI + e * I, I) for e in range(E)]:
                done = 0
                while done < count:
                    blk, p0 = (first + done) // P, (first + done) % P
                    n = min(P - p0, count - done)
                    sp.dma_start(stage_d[p0:p0 + n, blk, :], src[done:done + n, :]).then_inc(staged_d, 16)
                    done += n
                    down_parts += 1
            assert down_parts == DOWN_PARTS
            out_t = out.rearrange("b (s p) d -> p (b s) d", p=P)
            with sp.Fori(0, NT) as t:
                sp.wait_ge(res_done, t + 2)
                sp.dma_start(out_t[:, bass.ds(t, 1), :], resid[:, bass.ds(t, 1), :]).then_inc(stored, 16)
            sp.wait_ge(stored, 16 * NT)

        @block.tensor
        def _(pe):
            def transpose_xn(tile):
                pe.wait_ge(xn_done, tile + 1)
                for c in range(DC):
                    mm = pe.transpose(p_x[:, c, :], xn[:, c * P:(c + 1) * P], ident[:, :])
                mm.then_inc(xnt_ps, 1)

            def up(u):
                w = UP if u == 0 else UW
                for c in range(DC):
                    for n, (a, b) in enumerate(((1, 0), (0, 1), (0, 0))):
                        mm = pe.matmul(p_u[u % 4][:, 0:w], xnt[a][:, c, :], ups[b][:, u, c, 0:w],
                                       start=c == 0 and n == 0, stop=c == DC - 1 and n == 2)
                mm.then_inc(u_ps, 1)

            def transpose_acts(t, g):
                pe.wait_ge(act_done, t * NR + ready[g])
                for k, blk in enumerate(groups[g]):
                    r = rows[blk]
                    mm = pe.transpose(p_a[g % 2][0:r, k, :], acts[:, blk * P:blk * P + r], ident[:, :])
                mm.then_inc(a_ps, 1)

            def down(t, g):
                pe.wait_ge(a_lo, t * NG + g + 1)
                for k, blk in enumerate(groups[g]):
                    r = rows[blk]
                    for n, (a, b) in enumerate(((1, 0), (0, 1), (0, 0))):
                        mm = pe.matmul(p_y[:, :], actt[g % 2][a][0:r, k, :], downs[b][0:r, blk, :],
                                       start=blk == 0 and n == 0, stop=blk == NB - 1 and n == 2)
                if g == NG - 1:
                    mm.then_inc(y_ps, 1)

            pe.wait_ge(consts_in, 32)
            transpose_xn(0)
            pe.wait_ge(xnt_lo, 1)
            for u in range(3):
                pe.wait_ge(w_lo, u + 1)
                up(u)
            pe.wait_ge(w_lo, NU + 1)

            with pe.Fori(0, NT) as t:
                for u in range(3, NU):
                    if u >= 4:
                        pe.wait_ge(act_done, t * NR + read_by(u - 4))
                    up(u)
                    if u == 4:
                        transpose_acts(t, 0)
                    if u == 5:
                        pe.wait_ge(res_done, t + 1)
                        down(t, 0)
                    if u == 7:
                        transpose_acts(t, 1)
                    if u == 8:
                        transpose_xn(t + 1)
                transpose_acts(t, 2)
                down(t, 1)
                pe.wait_ge(xnt_lo, t + 2)
                pe.wait_ge(act_done, t * NR + read_by(8))
                up(0)
                transpose_acts(t, 3)
                up(1)
                down(t, 2)
                up(2)
                down(t, 3)

        @block.vector
        def _(dve):
            def norm_stats(tile):
                nc.vector.bn_stats(stats[:, :], resid[:, bass.ds(tile, 1), :]).then_inc(stats_done, 1)

            def norm_mv(count):
                dve.wait_ge(stats_done, count)
                dve.nop(nofuse=True)
                nc.vector.bn_aggr(mv[:, :], stats[:, :]).then_inc(mv_done, 1)

            def norm_x(count, tile):
                dve.wait_ge(rstd_done, count)
                nc.vector.tensor_scalar(xn[:, :].rearrange("p (o d) -> p o d", o=1), resid[:, bass.ds(tile, 1), :], mv[:, 0:1],
                                        rstd[:, 0:1], ALU.subtract, ALU.mult).then_inc(xn_done, 1)

            def xnt_low(count):
                dve.wait_ge(xnt_hi, count)
                nc.vector.tensor_tensor(xnt[1][:, :, :], p_x[:, :, :], xnt[0][:, :, :],
                                        ALU.subtract).then_inc(xnt_lo, 1)

            def route(tile):
                base = tile * RS

                def step(k, op):
                    op.then_inc(router, 1)
                    dve.wait_ge(router, base + k)
                    if k == 1:
                        dve.nop(nofuse=True)

                dve.wait_ge(silu_done, tile * NR + 1)
                step(1, nc.vector.tensor_copy(logit[:, :], p_u[0][:, UW:UP]))
                step(2, nc.vector.max(top[:, :], logit[:, :]))
                nc.vector.tensor_tensor(gap[:, :], top[:, 0:1], top[:, 1:2], ALU.subtract).then_inc(gap_done, 1)
                other = logit[:, None, :].to_broadcast([P, E, E])
                own = logit[:, :, None].to_broadcast([P, E, E])
                nc.vector.tensor_tensor(above[:, :, :], other, own, ALU.is_gt)
                step(3, nc.vector.tensor_tensor(equal[:, :, :], other, own, ALU.is_equal))
                step(4, nc.vector.tensor_tensor(equal[:, :, :], equal[:, :, :], before[:, :, :], ALU.mult))
                step(5, nc.vector.tensor_tensor(above[:, :, :], above[:, :, :], equal[:, :, :], ALU.add))
                nc.vector.tensor_reduce(rank[:, :], above[:, :, :], AX.X, ALU.add)
                dve.wait_ge(th_done, tile + 1)
                nc.vector.tensor_scalar(wtop[:, 0:1], th[:, :], 0.5, 0.5, ALU.mult, ALU.add)
                step(6, nc.vector.tensor_scalar(wtop[:, 1:2], th[:, :], -0.5, 0.5, ALU.mult, ALU.add))
                nc.vector.tensor_scalar(wfirst[:, :], rank[:, :], 0.0, wtop[:, 0:1], ALU.is_equal, ALU.mult)
                step(7, nc.vector.tensor_scalar(wt[:, :], rank[:, :], 1.0, wtop[:, 1:2], ALU.is_equal, ALU.mult))
                step(8, nc.vector.tensor_tensor(wt[:, :], wt[:, :], wfirst[:, :], ALU.add))

            def expert_act(base, e):
                r = 1 if e == 0 else e + 2
                bank = p_u[0 if e == 0 else (e + 2) % 4]
                dve.wait_ge(silu_done, base + r)
                c = SI + e * I
                nc.vector.scalar_tensor_tensor(acts[:, c:c + I], silu[:, e % 2, 0:I], wt[:, e:e + 1], bank[:, I:UW],
                                               ALU.mult, ALU.mult).then_inc(act_done, 1)

            def shared_act(base, ubase):
                dve.wait_ge(silu_done, base + 2)
                dve.wait_ge(u_ps, ubase + 3)
                nc.vector.tensor_tensor(acts[:, 0:SI], silu[:, 2, :], p_u[2][:, 0:UW], ALU.mult).then_inc(act_done, 1)

            def acts_low(t, g):
                dve.wait_ge(a_hi, t * NG + g + 1)
                for lo, hi, r in spans(g):
                    op = nc.vector.tensor_tensor(actt[g % 2][1][0:r, lo:hi, :], p_a[g % 2][0:r, lo:hi, :],
                                                 actt[g % 2][0][0:r, lo:hi, :], ALU.subtract)
                op.then_inc(a_lo, 1)

            nc.vector.memset(mhalf[:, :], -0.5).then_inc(res_done, 1)
            norm_stats(0)
            norm_mv(1)
            norm_x(1, 0)
            xnt_low(1)
            for u in range(NU):
                w = UP if u == 0 else UW
                dve.wait_ge(w_hi, u + 1)
                nc.vector.tensor_tensor(ups[1][:, u, :, 0:w], stage[:, u, :, 0:w], ups[0][:, u, :, 0:w],
                                        ALU.subtract).then_inc(w_lo, 1)
            dve.wait_ge(w_hi, NU + 1)
            for lo, hi, r in ((0, NB - 1, P), (NB - 1, NB, TAIL)):
                op = nc.vector.tensor_tensor(downs[1][0:r, lo:hi, :], stage_d[0:r, lo:hi, :], downs[0][0:r, lo:hi, :],
                                             ALU.subtract)
            op.then_inc(w_lo, 1)
            dve.wait_ge(consts_in, 32)
            route(0)
            expert_act(0, 0)
            shared_act(0, 0)

            with dve.Fori(0, NT) as t:
                nxt = (t + 1) % NT
                for e in range(1, E):
                    expert_act(t * NR, e)
                    if e == 1:
                        norm_stats(nxt)
                    if e == 2:
                        norm_mv(t + 2)
                        acts_low(t, 0)
                    if e == 4:
                        norm_x(t + 2, nxt)
                    if e == 5:
                        acts_low(t, 1)
                xnt_low(t + 2)
                acts_low(t, 2)
                route(t + 1)
                expert_act(t * NR + NR, 0)
                acts_low(t, 3)
                shared_act(t * NR + NR, t * NU + NU)
                dve.wait_ge(y_ps, t + 1)
                tile = resid[:, bass.ds(t, 1), :]
                nc.vector.tensor_tensor(tile, tile, p_y[:, :].rearrange("p (o d) -> p o d", o=1),
                                        ALU.add).then_inc(res_done, 1)

        @block.scalar
        def _(act):
            def gate(base, ubase, e):
                u = 0 if e == 0 else e + 2
                act.wait_ge(u_ps, ubase + u + 1)
                nc.scalar.activation(silu[:, e % 2, 0:I], p_u[u % 4][:, 0:I], ACT.Silu).then_inc(silu_done, 1)

            def shared_gate(ubase):
                act.wait_ge(u_ps, ubase + 2)
                nc.scalar.activation(silu[:, 2, :], p_u[1][:, 0:UW], ACT.Silu).then_inc(silu_done, 1)

            def tanh(tile):
                act.wait_ge(gap_done, tile + 1)
                nc.scalar.activation(th[:, :], gap[:, :], ACT.Tanh, scale=0.5).then_inc(th_done, 1)

            def acts_high(t, g):
                act.wait_ge(a_ps, t * NG + g + 1)
                for lo, hi, r in spans(g):
                    op = nc.scalar.copy(actt[g % 2][0][0:r, lo:hi, :], p_a[g % 2][0:r, lo:hi, :])
                op.then_inc(a_hi, 1)

            def xnt_high(count):
                act.wait_ge(xnt_ps, count)
                nc.scalar.copy(xnt[0][:, :, :], p_x[:, :, :]).then_inc(xnt_hi, 1)

            xnt_high(1)
            for u in range(NU):
                w = UP if u == 0 else UW
                act.wait_ge(staged[u], 64 if u == 0 else 32)
                nc.scalar.copy(ups[0][:, u, :, 0:w], stage[:, u, :, 0:w]).then_inc(w_hi, 1)
            act.wait_ge(staged_d, 16 * DOWN_PARTS)
            for lo, hi, r in ((0, NB - 1, P), (NB - 1, NB, TAIL)):
                op = nc.scalar.copy(downs[0][0:r, lo:hi, :], stage_d[0:r, lo:hi, :])
            op.then_inc(w_hi, 1)
            gate(0, 0, 0)
            tanh(0)
            shared_gate(0)

            with act.Fori(0, NT) as t:
                for e in range(1, E):
                    if e >= 2:
                        act.wait_ge(act_done, t * NR + (1 if e == 2 else e))
                    gate(t * NR, t * NU, e)
                    if e == 2:
                        acts_high(t, 0)
                    if e == 5:
                        acts_high(t, 1)
                xnt_high(t + 2)
                acts_high(t, 2)
                act.wait_ge(act_done, t * NR + 8)
                gate(t * NR + NR, t * NU + NU, 0)
                tanh(t + 1)
                acts_high(t, 3)
                shared_gate(t * NU + NU)

        @block.gpsimd
        def _(pool):
            def rsqrt(count):
                pool.wait_ge(mv_done, count)
                pool.nop(nofuse=True)
                nc.gpsimd.tensor_scalar(vare[:, :], mv[:, 1:2], EPS, 1.0, ALU.add, ALU.mult).then_inc(vare_done, 1)
                pool.wait_ge(vare_done, count)
                nc.gpsimd.tensor_tensor(rstd[:, :], vare[:, :], mhalf[:, :], ALU.pow).then_inc(rstd_done, 1)

            rsqrt(1)
            with pool.Fori(0, NT) as t:
                rsqrt(t + 2)


DOWN_PARTS = sum((first + count - 1) // P - first // P + 1
                 for first, count in [(0, SI)] + [(SI + e * I, I) for e in range(E)])


def build(nc, x, wq, wk, wv, wo, gate_w, w1, w3, w2, sw1, sw3, sw2, cos_t, sin_t, mask_t, ident_t,
          before_t, out):
    with nc.sbuf_tensor("resid", [P, NT, D], F32) as resid:
        attention_phase(nc, x, wq, wk, wv, wo, cos_t, sin_t, mask_t, ident_t, resid)
        experts_phase(nc, gate_w, w1, w3, w2, sw1, sw3, sw2, ident_t, before_t, resid, out)


def shape_constants():
    fraction = (np.float32(2.0) * np.arange(H // 2, dtype=np.float32)) / np.float32(H)
    timescale = np.power(np.float32(10000.0), fraction, dtype=np.float32)
    angle = np.arange(S, dtype=np.float32)[None, :] / timescale[:, None]
    cos, sin = np.cos(angle).astype(np.float32), np.sin(angle).astype(np.float32)
    row, col = np.arange(P)[:, None], np.arange(P)[None, :]
    diagonal = np.where(col <= row, 0.0, MASKED)
    return {
        "cos_t": np.concatenate([cos, cos]),
        "sin_t": np.concatenate([-sin, sin]),
        "mask_t": np.concatenate([np.zeros((P, P)), diagonal], axis=1).astype(np.float32),
        "ident_t": np.eye(P, dtype=np.float32),
        "before_t": np.broadcast_to(np.tril(np.ones((E, E), np.float32), -1), (P, E, E)).copy(),
    }


_INS = ["L0_attn_x", "L0_attn_wq", "L0_attn_wk", "L0_attn_wv", "L0_attn_wo", "L0_ffn_gate_w", "L0_ffn_w1",
        "L0_ffn_w3", "L0_ffn_w2", "L0_ffn_sw1", "L0_ffn_sw3", "L0_ffn_sw2"]


def kernel(**inputs):
    import concourse.bacc as _bacc
    from concourse.bass_utils import run_bass_kernel_spmd as _run

    nc = _bacc.Bacc("TRN2", target_bir_lowering=False, num_devices=1)
    arrays, args = {}, []
    for name, a in [(n, inputs[n]) for n in _INS] + list(shape_constants().items()):
        a = np.ascontiguousarray(a)
        arrays[f"in_{name}"] = a
        args.append(nc.dram_tensor(f"in_{name}", a.shape, mybir.dt.from_np(a.dtype), kind="ExternalInput").ap())
    args.append(nc.dram_tensor("out_x", (B, S, D), F32, kind="ExternalOutput").ap())
    build(nc, *args)
    r = _run(nc, [arrays], core_ids=[0])
    return r.results[0]["out_x"]
```

```python
from contextlib import ExitStack

import numpy as np

import concourse.bass as bass
from concourse import mybir

F32 = mybir.dt.float32
F32R = mybir.dt.float32r
ALU = mybir.AluOpType
ACT = mybir.ActivationFunctionType
AX = mybir.AxisListType

P = 128
B, S, D = 8, 256, 256
N, H = 16, 128
DC = D // P
ST = S // P
G, GH = 4, 4
GW = GH * H
NT = B * ST
E, I = 8, 176
SI = 2 * I
UW = 2 * I
AW = SI + E * I
NB = -(-AW // P)
TAIL = AW - (NB - 1) * P
EPS = 1e-5
MASKED = -1e30
SCALE = float(H) ** -0.5
BIG = 3.0e38
NSTAGE = 3
CH = 512
GE = 3 * DC * GW
NU = E + 2
UP = UW + E
NR = E + 1
RS = 8
GROUPS = [list(range(g, min(g + 4, NB))) for g in range(0, NB, 4)]
NG = len(GROUPS)


def rows_of(blk):
    return TAIL if blk == NB - 1 else P


def build(nc, x, wq, wk, wv, wo, gate_w, w1, w3, w2, sw1, sw3, sw2, cos_t, sin_t, mask_t, ident_t,
          before_t, out):
    ctx = ExitStack()
    with ctx:
        def sb(name, shape, dt=F32):
            return ctx.enter_context(nc.sbuf_tensor(name, shape, dt))

        def sem(name):
            return ctx.enter_context(nc.semaphore(name))

        resid = sb("resid", [P, NT, D])
        stage = sb("stage", [P, NSTAGE, CH])
        whl = [sb(f"w_{b}", [P, G * GE + N * D], F32R) for b in ("hi", "lo")]
        ident = sb("ident", [P, P])
        xn = sb("xn", [P, ST, D])
        xnt_all = [sb(f"xnt_{b}", [P, DC * S], F32R) for b in ("hi", "lo")]
        work = sb("work", [P, 3840])
        vbuf = [[sb(f"v_{b}{a}", [P, ST * GW], F32R) for b in ("hi", "lo")] for a in range(2)]
        cosn = sb("cosn", [P, S])
        sinn = sb("sinn", [P, S])
        mask = sb("mask", [P, S])
        qkt = [[sb(f"qkt_{b}{a}", [P, 2, S], F32R) for b in ("hi", "lo")] for a in range(2)]
        pts = [sb(f"pt_{b}", [P, 4, P], F32R) for b in ("hi", "lo")]
        att = [[sb(f"att_{b}{a}", [P, S], F32R) for b in ("hi", "lo")] for a in range(2)]
        stats = sb("stats", [P, ST, 6])
        mv = sb("mv", [P, ST, 2])
        vare = sb("vare", [P, ST])
        rstd = sb("rstd", [P, ST])
        mhalf = sb("mhalf", [P, ST])
        bias = sb("bias", [P, 2, ST])
        rsum = sb("rsum", [P, 2, ST])
        rinv = sb("rinv", [P, 2, ST])
        before = sb("before", [P, E, E])
        logit = sb("logit", [P, E])
        top = sb("top", [P, 8])
        gap = sb("gap", [P, 1])
        th = sb("th", [P, 1])
        wtop = sb("wtop", [P, 2])
        above = sb("above", [P, E, E])
        equal = sb("equal", [P, E, E])
        rank = sb("rank", [P, E])
        wfirst = sb("wfirst", [P, E])
        wt = sb("wt", [P, E])

        def wqk(m, b, g):
            at = g * GE + m * DC * GW
            return whl[b][:, at:at + DC * GW].rearrange("p (c n h) -> p c n h", c=DC, n=GH)

        def wvs(b, g):
            at = g * GE + 2 * DC * GW
            return whl[b][:, at:at + DC * GW].rearrange("p (c m) -> p c m", c=DC)

        def wos(b):
            return whl[b][:, G * GE:].rearrange("p (n d) -> p n d", n=N)

        xnt = [t[:, :].rearrange("p (c s) -> p c s", c=DC) for t in xnt_all]
        rope_cos = work[:, 0:1024].rearrange("p (a c s) -> p a c s", a=2, c=2)
        rope_sin = work[:, 1024:2048].rearrange("p (a c s) -> p a c s", a=2, c=2)
        roped = work[:, 2048:3072].rearrange("p (a c s) -> p a c s", a=2, c=2)
        prob = [work[:, 3072 + 384 * a:3456 + 384 * a] for a in range(2)]
        vs = [[t[:, :].rearrange("p (k m) -> p k m", k=ST) for t in pair] for pair in vbuf]

        ups = [t[:, 0:NU * DC * UP].rearrange("p (u c m) -> p u c m", u=NU, c=DC) for t in whl]
        downs = [t[:, NU * DC * UP:NU * DC * UP + NB * D].rearrange("p (n d) -> p n d", n=NB) for t in whl]
        assert NU * DC * UP + NB * D <= G * GE
        xnt2 = [t[:, 0:DC * P].rearrange("p (c s) -> p c s", c=DC) for t in xnt_all]
        silu = work[:, 0:3 * SI].rearrange("p (a m) -> p a m", a=3)
        acts = work[:, 3 * SI:3 * SI + NB * P]
        actt = [[t[:, 0:4 * P].rearrange("p (k m) -> p k m", k=4) for t in pair] for pair in vbuf]

        bank = [ctx.enter_context(nc.psum_tensor(f"bank{a}", [P, 512], F32)) for a in range(8)]

        def cut(a, inner):
            return bank[a][:, :].rearrange("p (a b) -> p a b", b=inner)

        p_qk = [cut(0, S), cut(1, S)]
        p_v = bank[2]
        p_s = [cut(3, S), cut(4, S)]
        p_t = cut(5, P)
        p_o = cut(6, S)
        p_y = cut(7, D)
        p_u = [bank[0], bank[1], bank[2], bank[3]]
        p_x = cut(4, P)
        p_a = [cut(5, P), cut(6, P)]
        p_y2 = bank[7]

        x_in = sem("x_in")
        tables_in = sem("tables_in")
        before_in = sem("before_in")
        staged = [sem(f"staged{a}") for a in range(NSTAGE)]
        w_hi = sem("w_hi")
        w_lo = sem("w_lo")
        consts = sem("consts")
        stats_done = sem("stats_done")
        mv_done = sem("mv_done")
        vare_done = sem("vare_done")
        rstd_done = sem("rstd_done")
        xn_done = sem("xn_done")
        xnt_ps = sem("xnt_ps")
        xnt_hi = sem("xnt_hi")
        xnt_lo = sem("xnt_lo")
        resid_done = sem("resid_done")
        v_ps = sem("v_ps")
        v_hi = sem("v_hi")
        v_lo = sem("v_lo")
        qk_ps = sem("qk_ps")
        rope_mul = sem("rope_mul")
        rope_add = sem("rope_add")
        qkt_hi = sem("qkt_hi")
        qkt_lo = sem("qkt_lo")
        s_ps = sem("s_ps")
        max_done = [sem("max0"), sem("max1")]
        exp_done = [sem("exp0"), sem("exp1")]
        inv_done = sem("inv_done")
        prob_done = sem("prob_done")
        pt_ps = sem("pt_ps")
        pt_hi = sem("pt_hi")
        pt_lo = sem("pt_lo")
        o_ps = sem("o_ps")
        o_hi = sem("o_hi")
        o_lo = sem("o_lo")
        y_ps = sem("y_ps")
        stats2_done = sem("stats2_done")
        mv2_done = sem("mv2_done")
        vare2_done = sem("vare2_done")
        rstd2_done = sem("rstd2_done")
        xn2_done = sem("xn2_done")
        xnt2_ps = sem("xnt2_ps")
        xnt2_hi = sem("xnt2_hi")
        xnt2_lo = sem("xnt2_lo")
        gap_done = sem("gap_done")
        th_done = sem("th_done")
        y2_ps = sem("y2_ps")
        res_done = sem("res_done")
        stored = sem("stored")
        router = sem("router")
        u_ps = sem("u_ps")
        silu_done = sem("silu_done")
        act_done = sem("act_done")
        a_ps = sem("a_ps")
        a_hi = sem("a_hi")
        a_lo = sem("a_lo")

        pieces = []

        def staged_at(n):
            return stage[:, n % NSTAGE, :]

        def add_piece(loads, seen):
            pieces.append((loads, seen))

        def add_group(g):
            for m, w in enumerate((wq, wk)):
                for c in range(DC):
                    src = w[c * P:(c + 1) * P, g * GH:(g + 1) * GH, :].rearrange("p n h -> p (n h)")
                    dst = [wqk(m, b, g)[:, c].rearrange("p n (two j) -> p n two j", two=2) for b in range(2)]
                    add_piece([(lambda t: t, src)],
                              [(lambda t: t.rearrange("p (n j two) -> p n two j", two=2, j=H // 2), dst[0], dst[1])])
            for c in range(DC):
                src = wv[c * P:(c + 1) * P, g * GH:(g + 1) * GH, :].rearrange("p n h -> p (n h)")
                add_piece([(lambda t: t, src)], [(lambda t: t, wvs(0, g)[:, c], wvs(1, g)[:, c])])

        def add_output(g):
            for n in range(g * GH, (g + 1) * GH, 2):
                src = wo[n:n + 2].rearrange("n h d -> h n d")
                add_piece([(lambda t: t.rearrange("p (n d) -> p n d", n=2), src)],
                          [(lambda t: t.rearrange("p (n d) -> p n d", n=2), wos(0)[:, n:n + 2], wos(1)[:, n:n + 2])])

        add_group(0)
        add_group(1)
        add_output(0)
        add_group(2)
        add_output(1)
        add_group(3)
        add_output(2)
        add_output(3)
        NATT = len(pieces)
        for u in range(NU):
            for c in range(DC):
                rc = slice(c * P, (c + 1) * P)
                w = UP if u == 0 else UW
                if u in (1, 2):
                    loads = [(lambda t: t[:, 0:UW], (sw1, sw3)[u - 1][rc])]
                else:
                    e = max(0, u - 2)
                    loads = [(lambda t: t[:, 0:I], w1[e][rc]), (lambda t: t[:, I:UW], w3[e][rc])]
                if u == 0:
                    loads.append((lambda t: t[:, UW:UP], gate_w[:, rc].rearrange("e p -> p e")))
                add_piece(loads, [(lambda t, w=w: t[:, 0:w], ups[0][:, u, c, 0:w], ups[1][:, u, c, 0:w])])
        down_rows = [(sw2, 0, SI)] + [(w2[e], SI + e * I, I) for e in range(E)]
        for b0 in range(0, NB, 2):
            loads = []
            for k in range(2):
                lo_row, hi_row = (b0 + k) * P, min((b0 + k + 1) * P, AW)
                for src, first, count in down_rows:
                    a, z = max(first, lo_row), min(first + count, hi_row)
                    if a < z:
                        loads.append((lambda t, a=a - lo_row, z=z - lo_row, k=k: t[a:z, k * D:(k + 1) * D],
                                      src[a - first:z - first, :]))
            seen = []
            for k in range(2):
                r = rows_of(b0 + k)
                seen.append((lambda t, r=r, k=k: t[0:r, k * D:(k + 1) * D], downs[0][0:r, b0 + k], downs[1][0:r, b0 + k]))
            add_piece(loads, seen)
        NP = len(pieces)
        staged_count, total = [], [0] * NSTAGE
        for n, (loads, _) in enumerate(pieces):
            total[n % NSTAGE] += 16 * len(loads)
            staged_count.append(total[n % NSTAGE])

        def split_schedule():
            first = {0: 2, 1: 2, 2: 1, 3: 1, 4: 2, 5: 2, 6: 2, 7: 2, 8: 2, 12: 2}
            last = {h: 1 for h in range(4, 12)} | {12: 4, 13: 4, 14: 4, 15: 2}
            plan, n = {}, 14
            for h in range(N):
                plan["first", h] = list(range(n, n + first.get(h, 0)))
                n += first.get(h, 0)
            assert n == NATT
            for h in range(N):
                plan["last", h] = list(range(n, n + last.get(h, 0)))
                n += last.get(h, 0)
            plan["rest"] = list(range(n, NP))
            return plan

        plan = split_schedule()

        def split_now(b, h):
            return plan["first", h] if b is FIRST else plan["last", h] if b is LAST else []

        FIRST, LAST = 0, B - 1

        def wait(eng, s, value):
            if not isinstance(value, int) or value > 0:
                eng.wait_ge(s, value)

        block = ctx.enter_context(nc.Block())

        @block.sync
        def _(sp):
            x_t = x.rearrange("b (t p) d -> p (b t) d", p=P)
            sp.dma_start(resid[:, 0:ST, :], x_t[:, 0:ST, :]).then_inc(x_in, 16)
            sp.dma_start(ident[:, :], ident_t).then_inc(tables_in, 16)
            for n, (loads, _) in enumerate(pieces):
                if n >= NSTAGE:
                    sp.wait_ge(w_lo, n - NSTAGE + 1)
                for view, src in loads:
                    with nc.allow_non_contiguous_dma(reason="the router's 2048 weights are transposed"):
                        sp.dma_start(view(staged_at(n)), src).then_inc(staged[n % NSTAGE], 16)
                if n == 2:
                    for dst, src in ((cosn, cos_t), (sinn, sin_t), (mask, mask_t)):
                        sp.dma_start(dst[:, :], src).then_inc(tables_in, 16)
                if n == 14:
                    sp.dma_start(resid[:, ST:NT, :], x_t[:, ST:NT, :]).then_inc(x_in, 16)
                    sp.dma_start(before[:, :, :], before_t).then_inc(before_in, 16)
            out_t = out.rearrange("b (s p) d -> p (b s) d", p=P)
            with sp.Fori(0, NT) as t:
                sp.wait_ge(res_done, t + 2)
                sp.dma_start(out_t[:, bass.ds(t, 1), :], resid[:, bass.ds(t, 1), :]).then_inc(stored, 16)
            sp.wait_ge(stored, 16 * NT)

        @block.tensor
        def _(pe):
            def three(out, lhs, rhs, start, stop, more=False):
                for n, (a, b) in enumerate(((1, 0), (0, 1), (0, 0))):
                    mm = pe.matmul(out, lhs[a], rhs[b], start=start and n == 0, stop=stop and n == 2,
                                   skip_group_check=more)
                return mm

            def transpose_xn(b):
                pe.wait_ge(xn_done, b + 1)
                for c in range(DC):
                    for t in range(ST):
                        mm = pe.transpose(p_qk[0][:, c, t * P:(t + 1) * P],
                                          xn[:, t, c * P:(c + 1) * P], ident[:, :])
                mm.then_inc(xnt_ps, 1)

            def project(h):
                for m in range(2):
                    for c in range(DC):
                        w = [wqk(m, b, h // GH)[:, c, h % GH] for b in range(2)]
                        mm = three(p_qk[h % 2][:, m, :], w, [xnt[b][:, c] for b in range(2)],
                                   c == 0, c == DC - 1)
                mm.then_inc(qk_ps, 1)

            def values(unit, c):
                g, t = unit // 2, unit % 2
                mm = three(p_v[:, :], [xnt[b][:, c, t * P:(t + 1) * P] for b in range(2)],
                           [wvs(b, g)[:, c] for b in range(2)], c == 0, c == DC - 1)
                if c == DC - 1:
                    mm.then_inc(v_ps, 1)

            def scores(h):
                a = h % 2
                pe.matmul(p_s[a][:, 0, 0:P], roped[:, a, 0, 0:P], roped[:, a, 1, 0:P], start=True, stop=True)
                mm = three(p_s[a][:, 1, :], [qkt[a][b][:, 0, P:2 * P] for b in range(2)],
                           [qkt[a][b][:, 1, :] for b in range(2)], True, True)
                mm.then_inc(s_ps, 1)

            def transpose_probs(h):
                for slot, src in ((2, 0), (3, P), (1, 2 * P)):
                    mm = pe.transpose(p_t[:, slot, :], prob[h % 2][:, src:src + P], ident[:, :])
                mm.then_inc(pt_ps, 1)

            def attend(h):
                for k in range(ST):
                    v = [vs[h // GH % 2][b][:, k, h % GH * H:(h % GH + 1) * H] for b in range(2)]
                    pt = [pts[b][:, 2 * (1 - k):2 * (1 - k) + 2, :] for b in range(2)]
                    mm = three(p_o[:, h % 2, :], v, pt, k == 0, k == ST - 1)
                mm.then_inc(o_ps, 1)

            def output(h):
                for t in range(ST):
                    mm = three(p_y[:, t, :], [att[h % 2][b][:, t * P:(t + 1) * P] for b in range(2)],
                               [wos(b)[:, h, :] for b in range(2)], h == 0 and t == 0,
                               h == N - 1 and t == ST - 1, more=True)
                mm.then_inc(y_ps, 1)

            def sequence(b):
                j0 = b * N
                for h in range(N):
                    last = h == N - 1
                    pe.wait_ge(prob_done, j0 + h + 1)
                    transpose_probs(h)
                    if b is not LAST or h + 2 < N:
                        pe.wait_ge(qkt_lo, j0 + h + 3)
                        scores((h + 2) % N)
                    if b is not LAST or h + 4 < N:
                        if h == 12:
                            pe.wait_ge(xnt_lo, b + 2)
                        if b is FIRST and h in (0, 4, 8):
                            pe.wait_ge(w_lo, (12, 20, 28)[h // 4])
                        project((h + 4) % N)
                    unit = (2 + h // 2) % (2 * G)

                    def half_values():
                        if b is LAST and unit < 2:
                            return
                        if h % 2 == 0:
                            pe.wait_ge(v_lo, b * 8 + 2 + h // 2)
                        values(unit, h % 2)

                    if not last:
                        half_values()
                    if h == 11 and b is not LAST:
                        pe.wait_ge(rope_mul, j0 + 15)
                        transpose_xn(b + 1)
                    pe.wait_ge(pt_lo, j0 + h + 1)
                    if h % GH == 0:
                        pe.wait_ge(v_lo, b * 8 + 2 * (h // GH) + 2)
                    attend(h)
                    if last:
                        half_values()
                    if h >= 1:
                        pe.wait_ge(o_lo, j0 + h)
                        if h == 1:
                            wait(pe, resid_done, b)
                        if b is FIRST and h in (1, 5, 9, 13):
                            pe.wait_ge(w_lo, (14, 22, 30, 32)[h // 4])
                        output(h - 1)
                    if last:
                        pe.wait_ge(o_lo, j0 + N)
                        output(h)

            pe.wait_ge(tables_in, 64)
            transpose_xn(0)
            pe.wait_ge(xnt_lo, 1)
            pe.wait_ge(w_lo, 4)
            for h in range(4):
                if h >= 2:
                    pe.wait_ge(rope_mul, h - 1)
                project(h)
                if h < 2:
                    if h == 0:
                        pe.wait_ge(w_lo, 6)
                    else:
                        pe.wait_ge(v_lo, h)
                    for c in range(DC):
                        values(h, c)
                if h >= 2:
                    pe.wait_ge(qkt_lo, h - 1)
                    scores(h - 2)
            pe.wait_ge(consts, 2)

            sequence(FIRST)
            with pe.Fori(1, LAST) as b:
                sequence(b)
            sequence(LAST)

            def transpose_xn2(tile):
                pe.wait_ge(xn2_done, tile + 1)
                for c in range(DC):
                    mm = pe.transpose(p_x[:, c, :], xn[:, 0, c * P:(c + 1) * P], ident[:, :])
                mm.then_inc(xnt2_ps, 1)

            def up(u):
                w = UP if u == 0 else UW
                for c in range(DC):
                    mm = three(p_u[u % 4][:, 0:w], [xnt2[b][:, c, :] for b in range(2)],
                               [ups[b][:, u, c, 0:w] for b in range(2)], c == 0, c == DC - 1)
                mm.then_inc(u_ps, 1)

            def transpose_acts(t, g):
                pe.wait_ge(act_done, t * NR + ready[g])
                for k, blk in enumerate(GROUPS[g]):
                    r = rows_of(blk)
                    mm = pe.transpose(p_a[g % 2][0:r, k, :], acts[:, blk * P:blk * P + r], ident[:, :])
                mm.then_inc(a_ps, 1)

            def down(t, g):
                pe.wait_ge(a_lo, t * NG + g + 1)
                for k, blk in enumerate(GROUPS[g]):
                    r = rows_of(blk)
                    mm = three(p_y2[:, 0:D], [actt[g % 2][b][0:r, k, :] for b in range(2)],
                               [downs[b][0:r, blk, :] for b in range(2)], blk == 0, blk == NB - 1)
                if g == NG - 1:
                    mm.then_inc(y2_ps, 1)

            transpose_xn2(0)
            pe.wait_ge(xnt2_lo, 1)
            for u in range(3):
                pe.wait_ge(w_lo, NATT + DC * (u + 1))
                up(u)
            pe.wait_ge(w_lo, NP)

            with pe.Fori(0, NT) as t:
                for u in range(3, NU):
                    if u >= 4:
                        pe.wait_ge(act_done, t * NR + read_by(u - 4))
                    up(u)
                    if u == 4:
                        transpose_acts(t, 0)
                    if u == 6:
                        pe.wait_ge(res_done, t + 1)
                        down(t, 0)
                    if u == 7:
                        transpose_acts(t, 1)
                    if u == 8:
                        transpose_xn2(t + 1)
                transpose_acts(t, 2)
                down(t, 1)
                pe.wait_ge(xnt2_lo, t + 2)
                pe.wait_ge(act_done, t * NR + read_by(8))
                up(0)
                transpose_acts(t, 3)
                up(1)
                down(t, 2)
                up(2)
                down(t, 3)

        @block.vector
        def _(dve):
            def split_lo(n):
                _, seen = pieces[n]
                dve.wait_ge(w_hi, n + 1)
                for view, hi, lo in seen:
                    op = nc.vector.tensor_tensor(lo, view(staged_at(n)), hi, ALU.subtract)
                op.then_inc(w_lo, 1)

            def norm_stats(b):
                for t in range(ST):
                    op = nc.vector.bn_stats(stats[:, t, :], resid[:, b * ST + t, :])
                op.then_inc(stats_done, 1)

            def norm_mv(b):
                dve.wait_ge(stats_done, b + 1)
                dve.nop(nofuse=True)
                for t in range(ST):
                    op = nc.vector.bn_aggr(mv[:, t, :], stats[:, t, :])
                op.then_inc(mv_done, 1)

            def norm_x(b):
                dve.wait_ge(rstd_done, b + 1)
                for t in range(ST):
                    op = nc.vector.tensor_scalar(xn[:, t, :], resid[:, b * ST + t, :], mv[:, t, 0:1],
                                                 rstd[:, t:t + 1], ALU.subtract, ALU.mult)
                op.then_inc(xn_done, 1)

            def rope_cosines(h):
                a = h % 2
                c = cosn[:, None, :].to_broadcast([P, 2, S])
                nc.vector.tensor_tensor(rope_cos[:, a], p_qk[a][:, :, :], c, ALU.mult)

            def rope_sines(h):
                a = h % 2
                for lo, hi in ((0, 64), (64, 0)):
                    sn = sinn[lo:lo + 64, None, :].to_broadcast([64, 2, S])
                    op = nc.vector.tensor_tensor(rope_sin[lo:lo + 64, a], p_qk[a][hi:hi + 64, :, :], sn,
                                                 ALU.mult)
                op.then_inc(rope_mul, 1)

            def mask_and_max(h):
                a = h % 2
                for t, cols, keys, m in ((0, slice(0, P), slice(0, P), slice(P, 2 * P)),
                                         (1, slice(P, 3 * P), slice(0, S), slice(0, S))):
                    nc.vector.tensor_tensor_reduce(prob[a][:, cols], p_s[a][:, t, keys], mask[:, m], -SCALE, BIG,
                                                   ALU.add, ALU.min, bias[:, a, t:t + 1]).then_inc(max_done[t], 1)

            def invert(h):
                nc.vector.reciprocal(rinv[:, h % 2, :], rsum[:, h % 2, :]).then_inc(inv_done, 1)

            def value_lo(unit):
                v = vs[unit // 2 % 2]
                nc.vector.tensor_tensor(v[1][:, unit % 2, :], p_v[:, :], v[0][:, unit % 2, :],
                                        ALU.subtract).then_inc(v_lo, 1)

            def probs_lo():
                nc.vector.tensor_tensor(pts[1][:, 1:4, :], p_t[:, 1:4, :], pts[0][:, 1:4, :],
                                        ALU.subtract).then_inc(pt_lo, 1)

            def att_lo(h):
                a = h % 2
                nc.vector.tensor_tensor(att[a][1][:, :], p_o[:, a, :], att[a][0][:, :],
                                        ALU.subtract).then_inc(o_lo, 1)

            def xnt_low(b):
                dve.wait_ge(xnt_hi, b + 1)
                nc.vector.tensor_tensor(xnt[1][:, :, :], p_qk[0][:, :, :], xnt[0][:, :, :],
                                        ALU.subtract).then_inc(xnt_lo, 1)

            def sequence(b):
                j0 = b * N
                for h in range(N):
                    dve.wait_ge(pt_hi, j0 + h + 1)
                    probs_lo()
                    if b is not LAST or h + 1 < N:
                        dve.wait_ge(exp_done[1], j0 + h + 2)
                        invert((h + 1) % N)
                    if b is not LAST or h + 2 < N:
                        dve.wait_ge(s_ps, j0 + h + 3)
                        dve.nop(nofuse=True)
                        mask_and_max((h + 2) % N)
                    if b is not LAST or h + 4 < N:
                        dve.wait_ge(qk_ps, j0 + h + 5)
                        dve.wait_ge(rope_add, j0 + h + 3)
                        rope_cosines((h + 4) % N)
                        rope_sines((h + 4) % N)
                    if h == 11 and b is not LAST:
                        xnt_low(b + 1)
                    if h % 2 == 1 and (b is not LAST or h < 12):
                        dve.wait_ge(v_hi, b * 8 + 3 + h // 2)
                        value_lo((2 + h // 2) % 8)
                    dve.wait_ge(o_hi, j0 + h + 1)
                    att_lo(h)
                    if b is not LAST:
                        if h == 4:
                            if b is FIRST:
                                dve.wait_ge(x_in, 32)
                            norm_stats(b + 1)
                        if h == 5:
                            norm_mv(b + 1)
                        if h == 8:
                            norm_x(b + 1)
                    else:
                        if h == 12:
                            norm2_stats(0)
                        if h == 13:
                            norm2_mv(1)
                        if h == 14:
                            norm2_x(1, 0)
                    for n in split_now(b, h):
                        split_lo(n)
                dve.wait_ge(y_ps, j0 + N)
                here = resid[:, bass.ds(b * ST, ST), :]
                op = nc.vector.tensor_tensor(here, here, p_y[:, :, :], ALU.add)
                op.then_inc(res_done if b is LAST else resid_done, 1)

            def norm2_stats(tile):
                nc.vector.bn_stats(stats[:, 0, :], resid[:, bass.ds(tile, 1), :]).then_inc(stats2_done, 1)

            def norm2_mv(count):
                dve.wait_ge(stats2_done, count)
                dve.nop(nofuse=True)
                nc.vector.bn_aggr(mv[:, 0, :], stats[:, 0, :]).then_inc(mv2_done, 1)

            def norm2_x(count, tile):
                dve.wait_ge(rstd2_done, count)
                nc.vector.tensor_scalar(xn[:, 0:1, :], resid[:, bass.ds(tile, 1), :], mv[:, 0, 0:1],
                                        rstd[:, 0:1], ALU.subtract, ALU.mult).then_inc(xn2_done, 1)

            nc.vector.memset(mhalf[:, :], -0.5)
            for b in range(2):
                op = nc.vector.memset(pts[b][:, 0, :].bitcast(F32), 0.0)
            op.then_inc(consts, 2)
            dve.wait_ge(x_in, 16)
            norm_stats(0)
            norm_mv(0)
            norm_x(0)
            xnt_low(0)
            for n in range(6):
                split_lo(n)
            for h in range(4):
                dve.wait_ge(qk_ps, h + 1)
                if h >= 2:
                    dve.wait_ge(rope_add, h - 1)
                rope_cosines(h)
                rope_sines(h)
                if h < 2:
                    dve.wait_ge(v_hi, h + 1)
                    value_lo(h)
                if h >= 2:
                    dve.wait_ge(s_ps, h - 1)
                    mask_and_max(h - 2)
                for n in range(6 + 2 * h, 8 + 2 * h):
                    split_lo(n)
            dve.wait_ge(exp_done[1], 1)
            invert(0)
            sequence(FIRST)
            with dve.Fori(1, LAST) as b:
                sequence(b)
            sequence(LAST)

            def xnt2_low(count):
                dve.wait_ge(xnt2_hi, count)
                nc.vector.tensor_tensor(xnt2[1][:, :, :], p_x[:, 0:DC, :], xnt2[0][:, :, :],
                                        ALU.subtract).then_inc(xnt2_lo, 1)

            def route(tile, meanwhile=lambda: None):
                def step(k, op):
                    op.then_inc(router, 1)
                    dve.wait_ge(router, tile * RS + k)
                    if k == 1:
                        dve.nop(nofuse=True)

                dve.wait_ge(silu_done, tile * NR + 1)
                step(1, nc.vector.tensor_copy(logit[:, :], p_u[0][:, UW:UP]))
                step(2, nc.vector.max(top[:, :], logit[:, :]))
                nc.vector.tensor_tensor(gap[:, :], top[:, 0:1], top[:, 1:2], ALU.subtract).then_inc(gap_done, 1)
                other = logit[:, None, :].to_broadcast([P, E, E])
                own = logit[:, :, None].to_broadcast([P, E, E])
                nc.vector.tensor_tensor(above[:, :, :], other, own, ALU.is_gt)
                step(3, nc.vector.tensor_tensor(equal[:, :, :], other, own, ALU.is_equal))
                step(4, nc.vector.tensor_tensor(equal[:, :, :], equal[:, :, :], before[:, :, :], ALU.mult))
                step(5, nc.vector.tensor_tensor(above[:, :, :], above[:, :, :], equal[:, :, :], ALU.add))
                nc.vector.tensor_reduce(rank[:, :], above[:, :, :], AX.X, ALU.add)
                meanwhile()
                dve.wait_ge(th_done, tile + 1)
                nc.vector.tensor_scalar(wtop[:, 0:1], th[:, :], 0.5, 0.5, ALU.mult, ALU.add)
                step(6, nc.vector.tensor_scalar(wtop[:, 1:2], th[:, :], -0.5, 0.5, ALU.mult, ALU.add))
                nc.vector.tensor_scalar(wfirst[:, :], rank[:, :], 0.0, wtop[:, 0:1], ALU.is_equal, ALU.mult)
                step(7, nc.vector.tensor_scalar(wt[:, :], rank[:, :], 1.0, wtop[:, 1:2], ALU.is_equal, ALU.mult))
                step(8, nc.vector.tensor_tensor(wt[:, :], wt[:, :], wfirst[:, :], ALU.add))

            def expert_act(base, e):
                u = 0 if e == 0 else e + 2
                dve.wait_ge(silu_done, base + (1 if e == 0 else e + 2))
                c = SI + e * I
                nc.vector.scalar_tensor_tensor(acts[:, c:c + I], silu[:, e % 2, 0:I], wt[:, e:e + 1],
                                               p_u[u % 4][:, I:UW], ALU.mult, ALU.mult).then_inc(act_done, 1)

            def shared_act(base, ubase):
                dve.wait_ge(silu_done, base + 2)
                dve.wait_ge(u_ps, ubase + 3)
                nc.vector.tensor_tensor(acts[:, 0:SI], silu[:, 2, :], p_u[2][:, 0:UW], ALU.mult).then_inc(act_done, 1)

            def acts_low(t, g):
                dve.wait_ge(a_hi, t * NG + g + 1)
                for lo, hi, r in spans(g):
                    op = nc.vector.tensor_tensor(actt[g % 2][1][0:r, lo:hi, :], p_a[g % 2][0:r, lo:hi, :],
                                                 actt[g % 2][0][0:r, lo:hi, :], ALU.subtract)
                op.then_inc(a_lo, 1)

            xnt2_low(1)
            for n in plan["rest"]:
                split_lo(n)
            dve.wait_ge(before_in, 16)
            route(0)
            expert_act(0, 0)
            shared_act(0, 0)

            with dve.Fori(0, NT) as t:
                nxt = (t + 1) % NT
                for e in range(1, E):
                    expert_act(t * NR, e)
                    if e == 1:
                        norm2_stats(nxt)
                    if e == 2:
                        acts_low(t, 0)
                        norm2_mv(t + 2)
                    if e == 4:
                        norm2_x(t + 2, nxt)
                    if e == 5:
                        acts_low(t, 1)
                xnt2_low(t + 2)
                acts_low(t, 2)
                route(t + 1, lambda: acts_low(t, 3))
                expert_act(t * NR + NR, 0)
                shared_act(t * NR + NR, t * NU + NU)
                dve.wait_ge(y2_ps, t + 1)
                tile = resid[:, bass.ds(t, 1), :]
                nc.vector.tensor_tensor(tile, tile, p_y[:, 0:1, :], ALU.add).then_inc(res_done, 1)

        @block.scalar
        def _(act):
            def split_hi(n):
                _, seen = pieces[n]
                act.wait_ge(staged[n % NSTAGE], staged_count[n])
                for view, hi, lo in seen:
                    op = nc.scalar.copy(hi, view(staged_at(n)))
                op.then_inc(w_hi, 1)

            def values_hi(unit):
                nc.scalar.copy(vs[unit // 2 % 2][0][:, unit % 2, :], p_v[:, :]).then_inc(v_hi, 1)

            def qkt_high(h):
                a = h % 2
                nc.scalar.copy(qkt[a][0][:, :, :], roped[:, a]).then_inc(qkt_hi, 1)

            def exps(j, h):
                a = h % 2
                for t, c in ((0, slice(0, P)), (1, slice(P, 3 * P))):
                    act.wait_ge(max_done[t], j + 1)
                    nc.scalar.activation(prob[a][:, c], prob[a][:, c], ACT.Exp, bias=bias[:, a, t:t + 1], scale=-1.0,
                                         accum_out=rsum[:, a, t:t + 1]).then_inc(exp_done[t], 1)

            def normalise(h):
                a = h % 2
                nc.scalar.activation(prob[a][:, 0:P], prob[a][:, 0:P], ACT.Copy, scale=rinv[:, a, 0:1])
                nc.scalar.activation(prob[a][:, P:3 * P], prob[a][:, P:3 * P], ACT.Copy,
                                     scale=rinv[:, a, 1:2]).then_inc(prob_done, 1)

            def xnt_high(b):
                act.wait_ge(xnt_ps, b + 1)
                nc.scalar.copy(xnt[0][:, :, :], p_qk[0][:, :, :]).then_inc(xnt_hi, 1)

            def sequence(b):
                j0 = b * N
                for h in range(N):
                    act.wait_ge(pt_ps, j0 + h + 1)
                    nc.scalar.copy(pts[0][:, 1:4, :], p_t[:, 1:4, :]).then_inc(pt_hi, 1)
                    if b is not LAST or h + 3 < N:
                        act.wait_ge(rope_add, j0 + h + 4)
                        qkt_high((h + 3) % N)
                    if b is not LAST or h + 1 < N:
                        act.wait_ge(inv_done, j0 + h + 2)
                        normalise((h + 1) % N)
                    if b is not LAST or h + 2 < N:
                        exps(j0 + h + 2, (h + 2) % N)
                    if h == 11 and b is not LAST:
                        xnt_high(b + 1)
                    if h % 2 == 1 and (b is not LAST or h < 12):
                        act.wait_ge(v_ps, b * 8 + 3 + h // 2)
                        values_hi((2 + h // 2) % 8)
                    act.wait_ge(o_ps, j0 + h + 1)
                    nc.scalar.copy(att[h % 2][0][:, :], p_o[:, h % 2, :]).then_inc(o_hi, 1)
                    for n in split_now(b, h):
                        split_hi(n)

            xnt_high(0)
            for n in range(6):
                split_hi(n)
            for h in range(4):
                if h < 2:
                    act.wait_ge(v_ps, h + 1)
                    values_hi(h)
                if h < 3:
                    act.wait_ge(rope_add, h + 1)
                    if h == 2:
                        act.wait_ge(s_ps, 1)
                    qkt_high(h)
                if h >= 2:
                    exps(h - 2, h - 2)
                for n in range(6 + 2 * h, 8 + 2 * h):
                    split_hi(n)
            act.wait_ge(inv_done, 1)
            normalise(0)
            sequence(FIRST)
            with act.Fori(1, LAST) as b:
                sequence(b)
            sequence(LAST)

            def gate(base, ubase, e):
                u = 0 if e == 0 else e + 2
                act.wait_ge(u_ps, ubase + u + 1)
                nc.scalar.activation(silu[:, e % 2, 0:I], p_u[u % 4][:, 0:I], ACT.Silu).then_inc(silu_done, 1)

            def shared_gate(ubase):
                act.wait_ge(u_ps, ubase + 2)
                nc.scalar.activation(silu[:, 2, :], p_u[1][:, 0:UW], ACT.Silu).then_inc(silu_done, 1)

            def tanh(tile):
                act.wait_ge(gap_done, tile + 1)
                nc.scalar.activation(th[:, :], gap[:, :], ACT.Tanh, scale=0.5).then_inc(th_done, 1)

            def acts_high(t, g):
                act.wait_ge(a_ps, t * NG + g + 1)
                for lo, hi, r in spans(g):
                    op = nc.scalar.copy(actt[g % 2][0][0:r, lo:hi, :], p_a[g % 2][0:r, lo:hi, :])
                op.then_inc(a_hi, 1)

            def xnt2_high(count):
                act.wait_ge(xnt2_ps, count)
                nc.scalar.copy(xnt2[0][:, :, :], p_x[:, 0:DC, :]).then_inc(xnt2_hi, 1)

            xnt2_high(1)
            for n in plan["rest"]:
                split_hi(n)
            gate(0, 0, 0)
            tanh(0)
            shared_gate(0)

            with act.Fori(0, NT) as t:
                for e in range(1, E):
                    if e >= 2:
                        act.wait_ge(act_done, t * NR + (1 if e == 2 else e))
                    gate(t * NR, t * NU, e)
                    if e == 2:
                        acts_high(t, 0)
                    if e == 5:
                        acts_high(t, 1)
                xnt2_high(t + 2)
                acts_high(t, 2)
                act.wait_ge(act_done, t * NR + 8)
                gate(t * NR + NR, t * NU + NU, 0)
                tanh(t + 1)
                acts_high(t, 3)
                shared_gate(t * NU + NU)

        @block.gpsimd
        def _(pool):
            def rsqrt(ready_sem, step_sem, done_sem, count, n):
                pool.wait_ge(ready_sem, count)
                pool.nop(nofuse=True)
                nc.gpsimd.tensor_scalar(vare[:, 0:n], mv[:, 0:n, 1], EPS, 1.0, ALU.add, ALU.mult).then_inc(step_sem, 1)
                pool.wait_ge(step_sem, count)
                nc.gpsimd.tensor_tensor(rstd[:, 0:n], vare[:, 0:n], mhalf[:, 0:n], ALU.pow).then_inc(done_sem, 1)

            def add(h):
                a = h % 2
                nc.gpsimd.tensor_tensor(roped[:, a], rope_cos[:, a], rope_sin[:, a], ALU.add).then_inc(rope_add, 1)

            def low(h):
                a = h % 2
                nc.gpsimd.tensor_tensor(qkt[a][1][:, :, :], roped[:, a], qkt[a][0][:, :, :],
                                        ALU.subtract).then_inc(qkt_lo, 1)

            def sequence(b):
                j0 = b * N
                for h in range(N):
                    if b is not LAST or h + 3 < N:
                        pool.wait_ge(rope_mul, j0 + h + 4)
                        pool.wait_ge(s_ps, j0 + h + 2)
                        add((h + 3) % N)
                        pool.wait_ge(qkt_hi, j0 + h + 4)
                        low((h + 3) % N)
                    if h == 5 and b is not LAST:
                        rsqrt(mv_done, vare_done, rstd_done, b + 2, ST)

            rsqrt(mv_done, vare_done, rstd_done, 1, ST)
            for h in range(3):
                pool.wait_ge(rope_mul, h + 1)
                if h == 2:
                    pool.wait_ge(s_ps, 1)
                add(h)
                pool.wait_ge(qkt_hi, h + 1)
                low(h)
            sequence(FIRST)
            with pool.Fori(1, LAST) as b:
                sequence(b)
            sequence(LAST)
            rsqrt(mv2_done, vare2_done, rstd2_done, 1, 1)
            with pool.Fori(0, NT) as t:
                rsqrt(mv2_done, vare2_done, rstd2_done, t + 2, 1)


ready = [2 + max(0, -(-(min(g[-1] * P + P, AW) - SI - I) // I)) for g in GROUPS]


def read_by(u):
    return (1, 2, 2)[u] if u < 3 else u


def spans(g):
    n = len(GROUPS[g])
    return [(0, n, P)] if g < NG - 1 or TAIL == P else [(0, n - 1, P), (n - 1, n, TAIL)]


def shape_constants():
    fraction = (np.float32(2.0) * np.arange(H // 2, dtype=np.float32)) / np.float32(H)
    timescale = np.power(np.float32(10000.0), fraction, dtype=np.float32)
    angle = np.arange(S, dtype=np.float32)[None, :] / timescale[:, None]
    cos, sin = np.cos(angle).astype(np.float32), np.sin(angle).astype(np.float32)
    row, col = np.arange(P)[:, None], np.arange(P)[None, :]
    diagonal = np.where(col <= row, 0.0, MASKED)
    return {
        "cos_t": np.concatenate([cos, cos]),
        "sin_t": np.concatenate([-sin, sin]),
        "mask_t": np.concatenate([np.zeros((P, P)), diagonal], axis=1).astype(np.float32),
        "ident_t": np.eye(P, dtype=np.float32),
        "before_t": np.broadcast_to(np.tril(np.ones((E, E), np.float32), -1), (P, E, E)).copy(),
    }


_INS = ["L0_attn_x", "L0_attn_wq", "L0_attn_wk", "L0_attn_wv", "L0_attn_wo", "L0_ffn_gate_w", "L0_ffn_w1",
        "L0_ffn_w3", "L0_ffn_w2", "L0_ffn_sw1", "L0_ffn_sw3", "L0_ffn_sw2"]


def kernel(**inputs):
    import concourse.bacc as _bacc
    from concourse.bass_utils import run_bass_kernel_spmd as _run

    nc = _bacc.Bacc("TRN2", target_bir_lowering=False, num_devices=1)
    arrays, args = {}, []
    for name, a in [(n, inputs[n]) for n in _INS] + list(shape_constants().items()):
        a = np.ascontiguousarray(a)
        arrays[f"in_{name}"] = a
        args.append(nc.dram_tensor(f"in_{name}", a.shape, mybir.dt.from_np(a.dtype), kind="ExternalInput").ap())
    args.append(nc.dram_tensor("out_x", (B, S, D), F32, kind="ExternalOutput").ap())
    build(nc, *args)
    r = _run(nc, [arrays], core_ids=[0])
    return r.results[0]["out_x"]
```

```python
from contextlib import ExitStack

import numpy as np

import concourse.bass as bass
from concourse import mybir

F32 = mybir.dt.float32
F32R = mybir.dt.float32r
ALU = mybir.AluOpType
ACT = mybir.ActivationFunctionType
AX = mybir.AxisListType

P = 128
B, S, D = 8, 256, 256
N, H = 16, 128
DC = D // P
ST = S // P
G, GH = 4, 4
GW = GH * H
NT = B * ST
E, I = 8, 176
SI = 2 * I
UW = 2 * I
AW = SI + E * I
NB = -(-AW // P)
TAIL = AW - (NB - 1) * P
EPS = 1e-5
MASKED = -1e30
SCALE = float(H) ** -0.5
BIG = 3.0e38
NSTAGE = 6
CH = 512
EARLY = 6 * DC
X_AFTER = [15, 17, 19, 21, 23, 25, 27]
GE = 3 * DC * GW
NU = E + 2
UP = UW + E
NR = E + 1
RS = 8
GROUPS = [list(range(g, min(g + 4, NB))) for g in range(0, NB, 4)]
NG = len(GROUPS)


def rows_of(blk):
    return TAIL if blk == NB - 1 else P


def build(nc, x, wq, wk, wv, wo, gate_w, w1, w3, w2, sw1, sw3, sw2, cos_t, sin_t, mask_t, ident_t,
          before_t, out):
    ctx = ExitStack()
    with ctx:
        def sb(name, shape, dt=F32):
            return ctx.enter_context(nc.sbuf_tensor(name, shape, dt))

        def sem(name):
            return ctx.enter_context(nc.semaphore(name))

        resid = sb("resid", [P, NT, D])
        stage = sb("stage", [P, NSTAGE, CH])
        whl = [sb(f"w_{b}", [P, G * GE + N * D], F32R) for b in ("hi", "lo")]
        ident = sb("ident", [P, P])
        xn = sb("xn", [P, ST, D])
        xnt_all = [sb(f"xnt_{b}", [P, DC * S], F32R) for b in ("hi", "lo")]
        work = sb("work", [P, 3840])
        vbuf = [[sb(f"v_{b}{a}", [P, GW], F32R) for b in ("hi", "lo")] for a in range(2)]
        v_late = [sb(f"v_late{a}", [P, GW]) for a in range(2)]
        cosn = sb("cosn", [P, S])
        sinn = sb("sinn", [P, S])
        mask = sb("mask", [P, S])
        qkt = [[sb(f"qkt_{b}{a}", [P, 2, S], F32R) for b in ("hi", "lo")] for a in range(2)]
        pts = [sb(f"pt_{b}", [P, 2, P], F32R) for b in ("hi", "lo")]
        pt_late = sb("pt_late", [P, P])
        att = [[sb(f"att_{b}{a}", [P, S], F32R) for b in ("hi", "lo")] for a in range(2)]
        stats = sb("stats", [P, ST, 6])
        mv = sb("mv", [P, ST, 2])
        vare = sb("vare", [P, ST])
        rstd = sb("rstd", [P, ST])
        mhalf = sb("mhalf", [P, ST])
        bias = sb("bias", [P, 2, ST])
        rsum = sb("rsum", [P, 2, ST])
        rinv = sb("rinv", [P, 2, ST])
        before = sb("before", [P, E, E])
        logit = sb("logit", [P, E])
        top = sb("top", [P, 8])
        gap = sb("gap", [P, 1])
        th = sb("th", [P, 1])
        wtop = sb("wtop", [P, 2])
        rank = sb("rank", [P, E])
        wfirst = sb("wfirst", [P, E])
        wt = sb("wt", [P, E])

        def wqk(m, b, g):
            at = g * GE + m * DC * GW
            return whl[b][:, at:at + DC * GW].rearrange("p (c n h) -> p c n h", c=DC, n=GH)

        def wvs(b, g):
            at = g * GE + 2 * DC * GW
            return whl[b][:, at:at + DC * GW].rearrange("p (c m) -> p c m", c=DC)

        def wos(b):
            return whl[b][:, G * GE:].rearrange("p (n d) -> p n d", n=N)

        xnt = [t[:, :].rearrange("p (c s) -> p c s", c=DC) for t in xnt_all]
        rope_cos = work[:, 0:1024].rearrange("p (a c s) -> p a c s", a=2, c=2)
        rope_sin = work[:, 1024:2048].rearrange("p (a c s) -> p a c s", a=2, c=2)
        roped = work[:, 2048:3072].rearrange("p (a c s) -> p a c s", a=2, c=2)
        prob = [work[:, 3072 + 384 * a:3456 + 384 * a] for a in range(2)]

        ups = [t[:, 0:NU * DC * UP].rearrange("p (u c m) -> p u c m", u=NU, c=DC) for t in whl]
        downs = [t[:, NU * DC * UP:NU * DC * UP + NB * D].rearrange("p (n d) -> p n d", n=NB) for t in whl]
        assert NU * DC * UP + NB * D <= G * GE
        above = cosn[:, 0:E * E].rearrange("p (i j) -> p i j", i=E)
        equal = sinn[:, 0:E * E].rearrange("p (i j) -> p i j", i=E)
        xnt2 = [t[:, 0:DC * P].rearrange("p (c s) -> p c s", c=DC) for t in xnt_all]
        silu = work[:, 0:3 * SI].rearrange("p (a m) -> p a m", a=3)
        acts = work[:, 3 * SI:3 * SI + NB * P]
        actt = [[t[:, 0:4 * P].rearrange("p (k m) -> p k m", k=4) for t in pair] for pair in vbuf]

        bank = [ctx.enter_context(nc.psum_tensor(f"bank{a}", [P, 512], F32)) for a in range(8)]

        def cut(a, inner):
            return bank[a][:, :].rearrange("p (a b) -> p a b", b=inner)

        p_qk = [cut(0, S), cut(1, S)]
        p_v = bank[2]
        p_s = [cut(3, S), cut(4, S)]
        p_t = cut(5, P)
        p_o = cut(6, S)
        p_y = cut(7, D)
        p_u = [bank[0], bank[1], bank[2], bank[3]]
        p_x = cut(4, P)
        p_x0 = cut(2, P)
        p_a = [cut(5, P), cut(6, P)]
        p_y2 = bank[7]

        x_in = sem("x_in")
        x1_in = sem("x1_in")
        x_rest_in = sem("x_rest_in")
        ident_in = sem("ident_in")
        tables_in = sem("tables_in")
        before_in = sem("before_in")
        staged = [sem(f"staged{a}") for a in range(NSTAGE)]
        w_hi = sem("w_hi")
        w_lo = [sem("w_lo_dve"), sem("w_lo_pool")]
        stats_done = sem("stats_done")
        mv_done = sem("mv_done")
        vare_done = sem("vare_done")
        rstd_done = sem("rstd_done")
        xn_done = sem("xn_done")
        xnt_ps = sem("xnt_ps")
        xnt_hi = sem("xnt_hi")
        xnt_lo = sem("xnt_lo")
        resid_done = sem("resid_done")
        v_ps = sem("v_ps")
        v_hi = sem("v_hi")
        v_lo = sem("v_lo")
        qk_ps = sem("qk_ps")
        rope_mul = sem("rope_mul")
        rope_add = sem("rope_add")
        qkt_hi = sem("qkt_hi")
        qkt_lo = sem("qkt_lo")
        s_ps = sem("s_ps")
        max_done = [sem("max0"), sem("max1")]
        exp_done = [sem("exp0"), sem("exp1")]
        inv_done = sem("inv_done")
        prob_done = sem("prob_done")
        pt_ps = sem("pt_ps")
        pt_hi = sem("pt_hi")
        pt_lo = sem("pt_lo")
        o_ps = sem("o_ps")
        o_hi = sem("o_hi")
        o_lo = sem("o_lo")
        y_ps = sem("y_ps")
        stats2_done = sem("stats2_done")
        mv2_done = sem("mv2_done")
        vare2_done = sem("vare2_done")
        rstd2_done = sem("rstd2_done")
        xn2_done = sem("xn2_done")
        xnt2_ps = sem("xnt2_ps")
        xnt2_hi = sem("xnt2_hi")
        xnt2_lo = sem("xnt2_lo")
        gap_done = sem("gap_done")
        th_done = sem("th_done")
        y2_ps = sem("y2_ps")
        res_done = sem("res_done")
        stored = sem("stored")
        router = sem("router")
        u_ps = sem("u_ps")
        silu_done = sem("silu_done")
        act_done = sem("act_done")
        a_ps = sem("a_ps")
        a_hi = sem("a_hi")
        a_lo = sem("a_lo")

        pieces = []

        def lo_by(n):
            return int(n in (1, 3, 6, 8, 11) if n < EARLY + 2 else n % 2 == 0)

        def lo_count(n, who):
            return sum(lo_by(m) == who for m in range(n))

        def wait_pieces(eng, n):
            for who in range(2):
                wait(eng, w_lo[who], lo_count(n, who))

        def add_piece(loads, seen):
            pieces.append((loads, seen))

        def add_group(g):
            for m, w in enumerate((wq, wk)):
                for c in range(DC):
                    src = w[c * P:(c + 1) * P, g * GH:(g + 1) * GH, :].rearrange("p n h -> p (n h)")
                    dst = [wqk(m, b, g)[:, c].rearrange("p n (two j) -> p n two j", two=2) for b in range(2)]
                    add_piece([(lambda t: t, src)],
                              [(lambda t: t.rearrange("p (n j two) -> p n two j", two=2, j=H // 2), dst[0], dst[1])])
            for c in range(DC):
                src = wv[c * P:(c + 1) * P, g * GH:(g + 1) * GH, :].rearrange("p n h -> p (n h)")
                add_piece([(lambda t: t, src)], [(lambda t: t, wvs(0, g)[:, c], wvs(1, g)[:, c])])

        def add_output(g):
            for n in range(g * GH, (g + 1) * GH, 2):
                src = wo[n:n + 2].rearrange("n h d -> h n d")
                add_piece([(lambda t: t.rearrange("p (n d) -> p n d", n=2), src)],
                          [(lambda t: t.rearrange("p (n d) -> p n d", n=2), wos(0)[:, n:n + 2], wos(1)[:, n:n + 2])])

        add_group(0)
        add_group(1)
        add_output(0)
        add_group(2)
        add_output(1)
        add_group(3)
        add_output(2)
        add_output(3)
        NATT = len(pieces)
        for u in range(NU):
            for c in range(DC):
                rc = slice(c * P, (c + 1) * P)
                w = UP if u == 0 else UW
                if u in (1, 2):
                    loads = [(lambda t: t[:, 0:UW], (sw1, sw3)[u - 1][rc])]
                else:
                    e = max(0, u - 2)
                    loads = [(lambda t: t[:, 0:I], w1[e][rc]), (lambda t: t[:, I:UW], w3[e][rc])]
                if u == 0:
                    loads.append((lambda t: t[:, UW:UP], gate_w[:, rc].rearrange("e p -> p e")))
                add_piece(loads, [(lambda t, w=w: t[:, 0:w], ups[0][:, u, c, 0:w], ups[1][:, u, c, 0:w])])
        down_rows = [(sw2, 0, SI)] + [(w2[e], SI + e * I, I) for e in range(E)]
        for b0 in range(0, NB, 2):
            loads = []
            for k in range(2):
                lo_row, hi_row = (b0 + k) * P, min((b0 + k + 1) * P, AW)
                for src, first, count in down_rows:
                    a, z = max(first, lo_row), min(first + count, hi_row)
                    if a < z:
                        loads.append((lambda t, a=a - lo_row, z=z - lo_row, k=k: t[a:z, k * D:(k + 1) * D],
                                      src[a - first:z - first, :]))
            seen = []
            for k in range(2):
                r = rows_of(b0 + k)
                seen.append((lambda t, r=r, k=k: t[0:r, k * D:(k + 1) * D], downs[0][0:r, b0 + k], downs[1][0:r, b0 + k]))
            add_piece(loads, seen)
        NP = len(pieces)
        staged_count, total = [], [0] * NSTAGE
        for n, (loads, _) in enumerate(pieces):
            total[n % NSTAGE] += 16 * len(loads)
            staged_count.append(total[n % NSTAGE])

        def split_schedule():
            first = {0: 3, 1: 2, 2: 3} | {h: 2 for h in range(3, 9)}
            last = {h: 2 for h in range(11)} | {11: 1, 13: 1, 14: 1}
            plan, n = {}, EARLY
            for h in range(N):
                plan["first", h] = list(range(n, n + first.get(h, 0)))
                n += first.get(h, 0)
            assert n == NATT
            for h in range(N):
                plan["last", h] = list(range(n, n + last.get(h, 0)))
                n += last.get(h, 0)
            plan["rest"] = list(range(n, NP))
            return plan

        plan = split_schedule()

        def split_now(b, h):
            which = "first" if b is FIRST else "last" if b is LAST else None
            return plan.get((which, h), [])

        FIRST, LAST, LAST_TILE = 0, B - 1, NT - 1

        def wait(eng, s, value):
            if not isinstance(value, int) or value > 0:
                eng.wait_ge(s, value)

        def rope_sum(eng, h):
            a = h % 2
            eng.tensor_tensor(roped[:, a], rope_cos[:, a], rope_sin[:, a], ALU.add).then_inc(rope_add, 1)

        block = ctx.enter_context(nc.Block())

        @block.sync
        def _(sp):
            x_t = x.rearrange("b (t p) d -> p (b t) d", p=P)
            sp.dma_start(resid[:, 0:ST, :], x_t[:, 0:ST, :]).then_inc(x_in, 16)
            for n, (loads, _) in enumerate(pieces):
                if n >= NSTAGE:
                    m = n - NSTAGE
                    sp.wait_ge(w_lo[lo_by(m)], lo_count(m + 1, lo_by(m)))
                for view, src in loads:
                    with nc.allow_non_contiguous_dma(reason="the router's 2048 weights are transposed"):
                        sp.dma_start(view(stage[:, n % NSTAGE, :]), src).then_inc(staged[n % NSTAGE], 16)
                if n == 1:
                    sp.dma_start(ident[:, :], ident_t).then_inc(ident_in, 16)
                if n == 4:
                    for dst, src in ((cosn, cos_t), (sinn, sin_t), (mask, mask_t)):
                        sp.dma_start(dst[:, :], src).then_inc(tables_in, 16)
                if n in X_AFTER:
                    b = 1 + X_AFTER.index(n)
                    sp.dma_start(resid[:, b * ST:(b + 1) * ST, :], x_t[:, b * ST:(b + 1) * ST, :]).then_inc(
                        x1_in if b == 1 else x_rest_in, 16)
            sp.dma_start(before[:, :, :], before_t).then_inc(before_in, 16)
            out_t = out.rearrange("b (s p) d -> p (b s) d", p=P)
            with sp.Fori(0, NT) as t:
                sp.wait_ge(res_done, t + 2)
                sp.dma_start(out_t[:, bass.ds(t, 1), :], resid[:, bass.ds(t, 1), :]).then_inc(stored, 16)
            sp.wait_ge(stored, 16 * NT)

        @block.tensor
        def _(pe):
            def three(out, lhs, rhs, start, stop, more=False):
                for n, (a, b) in enumerate(((1, 0), (0, 1), (0, 0))):
                    mm = pe.matmul(out, lhs[a], rhs[b], start=start and n == 0, stop=stop and n == 2,
                                   skip_group_check=more)
                return mm

            def transpose_xn(b):
                pe.wait_ge(xn_done, b + 1)
                for c in range(DC):
                    for t in range(ST):
                        mm = pe.transpose(p_qk[0][:, c, t * P:(t + 1) * P],
                                          xn[:, t, c * P:(c + 1) * P], ident[:, :])
                mm.then_inc(xnt_ps, 1)

            def project(h):
                for m in range(2):
                    for c in range(DC):
                        w = [wqk(m, b, h // GH)[:, c, h % GH] for b in range(2)]
                        mm = three(p_qk[h % 2][:, m, :], w, [xnt[b][:, c] for b in range(2)],
                                   c == 0, c == DC - 1)
                mm.then_inc(qk_ps, 1)

            def values(unit, c):
                g, t = unit // 2, unit % 2
                mm = three(p_v[:, :], [xnt[b][:, c, t * P:(t + 1) * P] for b in range(2)],
                           [wvs(b, g)[:, c] for b in range(2)], c == 0, c == DC - 1)
                if c == DC - 1:
                    mm.then_inc(v_ps, 1)

            def scores(h):
                a = h % 2
                pe.matmul(p_s[a][:, 0, 0:P], roped[:, a, 0, 0:P], roped[:, a, 1, 0:P], start=True, stop=True)
                mm = three(p_s[a][:, 1, :], [qkt[a][b][:, 0, P:2 * P] for b in range(2)],
                           [qkt[a][b][:, 1, :] for b in range(2)], True, True)
                mm.then_inc(s_ps, 1)

            def transpose_probs(h):
                for k in range(3):
                    mm = pe.transpose(p_t[:, k, :], prob[h % 2][:, k * P:(k + 1) * P], ident[:, :])
                mm.then_inc(pt_ps, 1)

            def attend(h):
                g, cols = h // GH % 2, slice(h % GH * H, (h % GH + 1) * H)
                three(p_o[:, h % 2, :], [vbuf[g][b][:, cols] for b in range(2)],
                      [pts[b][:, :, :] for b in range(2)], True, False)
                pe.matmul(p_o[:, h % 2, P:2 * P], v_late[g][:, cols], pt_late[:, :], start=False,
                          stop=True).then_inc(o_ps, 1)

            def output(h):
                for t in range(ST):
                    mm = three(p_y[:, t, :], [att[h % 2][b][:, t * P:(t + 1) * P] for b in range(2)],
                               [wos(b)[:, h, :] for b in range(2)], h == 0 and t == 0,
                               h == N - 1 and t == ST - 1, more=True)
                mm.then_inc(y_ps, 1)

            def sequence(b):
                j0 = b * N
                for h in range(N):
                    pe.wait_ge(prob_done, j0 + h + 1)
                    transpose_probs(h)
                    if b is not LAST or h + 2 < N:
                        pe.wait_ge(qkt_lo, j0 + h + 3)
                        scores((h + 2) % N)
                    if b is not LAST or h + 4 < N:
                        if h == 12:
                            pe.wait_ge(xnt_lo, b + 2)
                        if b is FIRST and h in (0, 4, 8):
                            wait_pieces(pe, (12, 20, 28)[h // 4])
                        project((h + 4) % N)
                    unit = (2 + h // 2) % (2 * G)

                    def half_values():
                        if b is LAST and unit < 2:
                            return
                        if h % 4 == 0:
                            pe.wait_ge(v_hi, b * 8 + 2 + h // 2)
                        if h % 4 == 2:
                            pe.wait_ge(v_lo, b * 4 + 2 + h // 4)
                        values(unit, h % 2)

                    half_values()
                    if b is LAST:
                        ahead(h)
                    if h == 11 and b is not LAST:
                        pe.wait_ge(rope_mul, j0 + 15)
                        transpose_xn(b + 1)
                    pe.wait_ge(pt_lo, j0 + h + 1)
                    if h % GH == 0:
                        pe.wait_ge(v_lo, b * 4 + h // GH + 1)
                        pe.wait_ge(v_hi, b * 8 + 2 * (h // GH) + 2)
                    attend(h)
                    if h >= 1 or b is not FIRST:
                        pe.wait_ge(o_lo, j0 + h)
                        if h == 1:
                            wait(pe, resid_done, b)
                        if b is FIRST and h in (1, 5, 9, 13):
                            wait_pieces(pe, (14, 22, 30, 32)[h // 4])
                        output((h - 1) % N)
                if b is LAST:
                    pe.wait_ge(o_lo, j0 + N)
                    output(N - 1)

            def ahead(h):
                if h == 12:
                    pe.wait_ge(v_hi, B * 8)
                    transpose_xn2(0, p_x0)
                if h == 13:
                    pe.wait_ge(xnt2_lo, 1)
                if h in (13, 14):
                    pe.wait_ge(rope_mul, B * N + h - 14)
                if h >= 13:
                    wait_pieces(pe, NATT + DC * (h - 12))
                    up(h - 13)

            def transpose_xn2(tile, dst=p_x):
                pe.wait_ge(xn2_done, tile + 1)
                for c in range(DC):
                    mm = pe.transpose(dst[:, c, :], xn[:, 0, c * P:(c + 1) * P], ident[:, :])
                mm.then_inc(xnt2_ps, 1)

            def up(u):
                w = UP if u == 0 else UW
                for c in range(DC):
                    mm = three(p_u[u % 4][:, 0:w], [xnt2[b][:, c, :] for b in range(2)],
                               [ups[b][:, u, c, 0:w] for b in range(2)], c == 0, c == DC - 1)
                mm.then_inc(u_ps, 1)

            def transpose_acts(t, g):
                pe.wait_ge(act_done, t * NR + ready[g])
                for k, blk in enumerate(GROUPS[g]):
                    r = rows_of(blk)
                    mm = pe.transpose(p_a[g % 2][0:r, k, :], acts[:, blk * P:blk * P + r], ident[:, :])
                mm.then_inc(a_ps, 1)

            def down(t, g):
                pe.wait_ge(a_lo, t * NG + g + 1)
                for k, blk in enumerate(GROUPS[g]):
                    r = rows_of(blk)
                    mm = three(p_y2[:, 0:D], [actt[g % 2][b][0:r, k, :] for b in range(2)],
                               [downs[b][0:r, blk, :] for b in range(2)], blk == 0, blk == NB - 1)
                if g == NG - 1:
                    mm.then_inc(y2_ps, 1)

            pe.wait_ge(ident_in, 16)
            transpose_xn(0)
            pe.wait_ge(xnt_lo, 1)
            wait_pieces(pe, 4)
            project(0)
            project(1)
            wait_pieces(pe, 6)
            for c in range(DC):
                values(0, c)
            for h in range(2):
                pe.wait_ge(qkt_lo, h + 1)
                scores(h)
                pe.wait_ge(rope_mul, h + 1)
                project(h + 2)
                if h == 0:
                    pe.wait_ge(v_lo, 1)
                    for c in range(DC):
                        values(1, c)

            sequence(FIRST)
            with pe.Fori(1, LAST) as b:
                sequence(b)
            sequence(LAST)

            wait_pieces(pe, NATT + DC * NU)

            def tile_step(t):
                more = t is not LAST_TILE
                for u in range(3, NU):
                    if u >= 4:
                        pe.wait_ge(act_done, t * NR + read_by(u - 4))
                    up(u)
                    if u == 4:
                        transpose_acts(t, 0)
                    if u == 6:
                        wait_pieces(pe, NP)
                        pe.wait_ge(res_done, t + 1)
                        down(t, 0)
                    if u == 7:
                        transpose_acts(t, 1)
                    if u == 8 and more:
                        transpose_xn2(t + 1)
                transpose_acts(t, 2)
                down(t, 1)
                if more:
                    pe.wait_ge(xnt2_lo, t + 2)
                    pe.wait_ge(act_done, t * NR + read_by(8))
                    up(0)
                transpose_acts(t, 3)
                if more:
                    up(1)
                down(t, 2)
                if more:
                    up(2)
                down(t, 3)

            with pe.Fori(0, LAST_TILE) as t:
                tile_step(t)
            tile_step(LAST_TILE)

        @block.vector
        def _(dve):
            def split_lo(n):
                _, seen = pieces[n]
                dve.wait_ge(w_hi, n + 1)
                for view, hi, lo in seen:
                    op = nc.vector.tensor_tensor(lo, view(stage[:, n % NSTAGE, :]), hi, ALU.subtract)
                op.then_inc(w_lo[0], 1)

            def norm_stats(b):
                for t in range(ST):
                    op = nc.vector.bn_stats(stats[:, t, :], resid[:, b * ST + t, :])
                op.then_inc(stats_done, 1)

            def norm_mv(b):
                dve.wait_ge(stats_done, b + 1)
                dve.nop(nofuse=True)
                for t in range(ST):
                    op = nc.vector.bn_aggr(mv[:, t, :], stats[:, t, :])
                op.then_inc(mv_done, 1)

            def norm_x(b):
                dve.wait_ge(rstd_done, b + 1)
                for t in range(ST):
                    op = nc.vector.tensor_scalar(xn[:, t, :], resid[:, b * ST + t, :], mv[:, t, 0:1],
                                                 rstd[:, t:t + 1], ALU.subtract, ALU.mult)
                op.then_inc(xn_done, 1)

            def rope_cosines(h):
                a = h % 2
                c = cosn[:, None, :].to_broadcast([P, 2, S])
                nc.vector.tensor_tensor(rope_cos[:, a], p_qk[a][:, :, :], c, ALU.mult)

            def rope_sines(h):
                a = h % 2
                for lo, hi in ((0, 64), (64, 0)):
                    sn = sinn[lo:lo + 64, None, :].to_broadcast([64, 2, S])
                    op = nc.vector.tensor_tensor(rope_sin[lo:lo + 64, a], p_qk[a][hi:hi + 64, :, :], sn,
                                                 ALU.mult)
                op.then_inc(rope_mul, 1)

            def mask_and_max(h):
                a = h % 2
                for t, cols, keys, m in ((0, slice(0, P), slice(0, P), slice(P, 2 * P)),
                                         (1, slice(P, 3 * P), slice(0, S), slice(0, S))):
                    nc.vector.tensor_tensor_reduce(prob[a][:, cols], p_s[a][:, t, keys], mask[:, m], -SCALE, BIG,
                                                   ALU.add, ALU.min, bias[:, a, t:t + 1]).then_inc(max_done[t], 1)

            def invert(h):
                nc.vector.reciprocal(rinv[:, h % 2, :], rsum[:, h % 2, :]).then_inc(inv_done, 1)

            def value_lo(g):
                v = vbuf[g % 2]
                nc.vector.tensor_tensor(v[1][:, :], p_v[:, :], v[0][:, :], ALU.subtract).then_inc(v_lo, 1)

            def probs_lo():
                nc.vector.tensor_tensor(pts[1][:, :, :], p_t[:, 0:2, :], pts[0][:, :, :],
                                        ALU.subtract).then_inc(pt_lo, 1)

            def att_lo(h):
                a = h % 2
                nc.vector.tensor_tensor(att[a][1][:, :], p_o[:, a, :], att[a][0][:, :],
                                        ALU.subtract).then_inc(o_lo, 1)

            def xnt_low(b):
                dve.wait_ge(xnt_hi, b + 1)
                nc.vector.tensor_tensor(xnt[1][:, :, :], p_qk[0][:, :, :], xnt[0][:, :, :],
                                        ALU.subtract).then_inc(xnt_lo, 1)

            def sequence(b):
                j0 = b * N
                for h in range(N):
                    dve.wait_ge(pt_hi, j0 + h + 1)
                    probs_lo()
                    if b is not LAST or h + 1 < N:
                        dve.wait_ge(exp_done[1], j0 + h + 2)
                        invert((h + 1) % N)
                    if b is not LAST or h + 2 < N:
                        dve.wait_ge(s_ps, j0 + h + 3)
                        dve.nop(nofuse=True)
                        mask_and_max((h + 2) % N)
                    if b is not LAST or h + 4 < N:
                        dve.wait_ge(qk_ps, j0 + h + 5)
                        dve.wait_ge(rope_add, j0 + h + 3)
                        rope_cosines((h + 4) % N)
                        rope_sines((h + 4) % N)
                    if h == 11 and b is not LAST:
                        xnt_low(b + 1)
                    if h % 4 == 1 and (b is not LAST or h < 12):
                        dve.wait_ge(v_hi, b * 8 + 3 + h // 2)
                        value_lo((h // GH + 1) % G)
                    dve.wait_ge(o_hi, j0 + h + 1)
                    att_lo(h)
                    if h == 0 and b is not FIRST:
                        residual(b - 1)
                    if b is not LAST:
                        if h == 4:
                            if b is FIRST:
                                dve.wait_ge(x1_in, 16)
                            else:
                                dve.wait_ge(x_rest_in, 16 * (B - 2))
                            norm_stats(b + 1)
                        if h == 5:
                            norm_mv(b + 1)
                        if h == 8:
                            norm_x(b + 1)
                    else:
                        if h == 4:
                            norm2_stats(0)
                        if h == 5:
                            norm2_mv(1)
                        if h == 8:
                            norm2_x(1, 0)
                        if h == 12:
                            xnt2_low(1, p_x0)
                    for n in split_now(b, h):
                        if lo_by(n) == 0:
                            split_lo(n)

            def residual(b):
                dve.wait_ge(y_ps, b * N + N)
                here = resid[:, bass.ds(b * ST, ST), :]
                op = nc.vector.tensor_tensor(here, here, p_y[:, :, :], ALU.add)
                op.then_inc(res_done if b is LAST else resid_done, 1)

            def norm2_stats(tile):
                nc.vector.bn_stats(stats[:, 0, :], resid[:, bass.ds(tile, 1), :]).then_inc(stats2_done, 1)

            def norm2_mv(count):
                dve.wait_ge(stats2_done, count)
                dve.nop(nofuse=True)
                nc.vector.bn_aggr(mv[:, 0, :], stats[:, 0, :]).then_inc(mv2_done, 1)

            def norm2_x(count, tile):
                dve.wait_ge(rstd2_done, count)
                nc.vector.tensor_scalar(xn[:, 0:1, :], resid[:, bass.ds(tile, 1), :], mv[:, 0, 0:1],
                                        rstd[:, 0:1], ALU.subtract, ALU.mult).then_inc(xn2_done, 1)

            def xnt2_low(count, src=p_x):
                dve.wait_ge(xnt2_hi, count)
                nc.vector.tensor_tensor(xnt2[1][:, :, :], src[:, 0:DC, :], xnt2[0][:, :, :],
                                        ALU.subtract).then_inc(xnt2_lo, 1)

            nc.vector.memset(mhalf[:, :], -0.5)
            dve.wait_ge(x_in, 16)
            norm_stats(0)
            norm_mv(0)
            split_lo(0)
            norm_x(0)
            split_lo(2)
            xnt_low(0)
            for n in (4, 5, 7):
                split_lo(n)

            def rope(h):
                dve.wait_ge(qk_ps, h + 1)
                rope_cosines(h)
                rope_sines(h)

            def early_max(h):
                dve.wait_ge(s_ps, h + 1)
                mask_and_max(h)

            dve.wait_ge(tables_in, 48)
            rope(0)
            dve.wait_ge(rope_mul, 1)
            rope_sum(nc.vector, 0)
            rope(1)
            split_lo(9)
            dve.wait_ge(v_hi, 1)
            value_lo(0)
            split_lo(10)
            early_max(0)
            dve.wait_ge(rope_add, 1)
            rope(2)
            dve.wait_ge(exp_done[1], 1)
            invert(0)
            early_max(1)
            dve.wait_ge(rope_add, 2)
            rope(3)
            sequence(FIRST)
            with dve.Fori(1, LAST) as b:
                sequence(b)
            sequence(LAST)

            def route(tile, meanwhile=lambda: None):
                def step(k, op):
                    op.then_inc(router, 1)
                    dve.wait_ge(router, tile * RS + k)
                    if k == 1:
                        dve.nop(nofuse=True)

                dve.wait_ge(silu_done, tile * NR + 1)
                step(1, nc.vector.tensor_copy(logit[:, :], p_u[0][:, UW:UP]))
                step(2, nc.vector.max(top[:, :], logit[:, :]))
                nc.vector.tensor_tensor(gap[:, :], top[:, 0:1], top[:, 1:2], ALU.subtract).then_inc(gap_done, 1)
                other = logit[:, None, :].to_broadcast([P, E, E])
                own = logit[:, :, None].to_broadcast([P, E, E])
                nc.vector.tensor_tensor(above[:, :, :], other, own, ALU.is_gt)
                step(3, nc.vector.tensor_tensor(equal[:, :, :], other, own, ALU.is_equal))
                step(4, nc.vector.tensor_tensor(equal[:, :, :], equal[:, :, :], before[:, :, :], ALU.mult))
                step(5, nc.vector.tensor_tensor(above[:, :, :], above[:, :, :], equal[:, :, :], ALU.add))
                nc.vector.tensor_reduce(rank[:, :], above[:, :, :], AX.X, ALU.add)
                meanwhile()
                dve.wait_ge(th_done, tile + 1)
                nc.vector.tensor_scalar(wtop[:, 0:1], th[:, :], 0.5, 0.5, ALU.mult, ALU.add)
                step(6, nc.vector.tensor_scalar(wtop[:, 1:2], th[:, :], -0.5, 0.5, ALU.mult, ALU.add))
                nc.vector.tensor_scalar(wfirst[:, :], rank[:, :], 0.0, wtop[:, 0:1], ALU.is_equal, ALU.mult)
                step(7, nc.vector.tensor_scalar(wt[:, :], rank[:, :], 1.0, wtop[:, 1:2], ALU.is_equal, ALU.mult))
                step(8, nc.vector.tensor_tensor(wt[:, :], wt[:, :], wfirst[:, :], ALU.add))

            def expert_act(base, e):
                u = 0 if e == 0 else e + 2
                dve.wait_ge(silu_done, base + (1 if e == 0 else e + 2))
                c = SI + e * I
                nc.vector.scalar_tensor_tensor(acts[:, c:c + I], silu[:, e % 2, 0:I], wt[:, e:e + 1],
                                               p_u[u % 4][:, I:UW], ALU.mult, ALU.mult).then_inc(act_done, 1)

            def shared_act(base, ubase):
                dve.wait_ge(silu_done, base + 2)
                dve.wait_ge(u_ps, ubase + 3)
                nc.vector.tensor_tensor(acts[:, 0:SI], silu[:, 2, :], p_u[2][:, 0:UW], ALU.mult).then_inc(act_done, 1)

            def acts_low(t, g):
                dve.wait_ge(a_hi, t * NG + g + 1)
                for lo, hi, r in spans(g):
                    op = nc.vector.tensor_tensor(actt[g % 2][1][0:r, lo:hi, :], p_a[g % 2][0:r, lo:hi, :],
                                                 actt[g % 2][0][0:r, lo:hi, :], ALU.subtract)
                op.then_inc(a_lo, 1)

            dve.wait_ge(before_in, 16)
            route(0)
            expert_act(0, 0)
            shared_act(0, 0)
            residual(LAST)
            for n in plan["rest"]:
                if lo_by(n) == 0:
                    split_lo(n)

            def tile_step(t):
                more = t is not LAST_TILE
                for e in range(1, E):
                    expert_act(t * NR, e)
                    if e == 1 and more:
                        norm2_stats(t + 1)
                    if e == 2:
                        acts_low(t, 0)
                        if more:
                            norm2_mv(t + 2)
                    if e == 4 and more:
                        norm2_x(t + 2, t + 1)
                    if e == 5:
                        acts_low(t, 1)
                if more:
                    xnt2_low(t + 2)
                acts_low(t, 2)
                if more:
                    route(t + 1, lambda: acts_low(t, 3))
                    expert_act(t * NR + NR, 0)
                    shared_act(t * NR + NR, t * NU + NU)
                else:
                    acts_low(t, 3)
                dve.wait_ge(y2_ps, t + 1)
                tile = resid[:, bass.ds(t, 1), :]
                nc.vector.tensor_tensor(tile, tile, p_y[:, 0:1, :], ALU.add).then_inc(res_done, 1)

            with dve.Fori(0, LAST_TILE) as t:
                tile_step(t)
            tile_step(LAST_TILE)

        @block.scalar
        def _(act):
            def split_hi(n):
                _, seen = pieces[n]
                act.wait_ge(staged[n % NSTAGE], staged_count[n])
                for view, hi, lo in seen:
                    op = nc.scalar.copy(hi, view(stage[:, n % NSTAGE, :]))
                op.then_inc(w_hi, 1)

            def values_hi(unit):
                dst = (vbuf[unit // 2 % 2][0], v_late[unit // 2 % 2])[unit % 2]
                nc.scalar.copy(dst[:, :], p_v[:, :]).then_inc(v_hi, 1)

            def qkt_high(h):
                a = h % 2
                nc.scalar.copy(qkt[a][0][:, :, :], roped[:, a]).then_inc(qkt_hi, 1)

            def exps(j, h):
                a = h % 2
                for t, c in ((0, slice(0, P)), (1, slice(P, 3 * P))):
                    act.wait_ge(max_done[t], j + 1)
                    nc.scalar.activation(prob[a][:, c], prob[a][:, c], ACT.Exp, bias=bias[:, a, t:t + 1], scale=-1.0,
                                         accum_out=rsum[:, a, t:t + 1]).then_inc(exp_done[t], 1)

            def normalise(h):
                a = h % 2
                nc.scalar.activation(prob[a][:, 0:P], prob[a][:, 0:P], ACT.Copy, scale=rinv[:, a, 0:1])
                nc.scalar.activation(prob[a][:, P:3 * P], prob[a][:, P:3 * P], ACT.Copy,
                                     scale=rinv[:, a, 1:2]).then_inc(prob_done, 1)

            def xnt_high(b):
                act.wait_ge(xnt_ps, b + 1)
                nc.scalar.copy(xnt[0][:, :, :], p_qk[0][:, :, :]).then_inc(xnt_hi, 1)

            def sequence(b):
                j0 = b * N
                for h in range(N):
                    act.wait_ge(pt_ps, j0 + h + 1)
                    nc.scalar.copy(pt_late[:, :], p_t[:, 2, :])
                    nc.scalar.copy(pts[0][:, :, :], p_t[:, 0:2, :]).then_inc(pt_hi, 1)
                    if b is not LAST or h + 3 < N:
                        act.wait_ge(rope_add, j0 + h + 4)
                        qkt_high((h + 3) % N)
                    if b is not LAST or h + 1 < N:
                        act.wait_ge(inv_done, j0 + h + 2)
                        normalise((h + 1) % N)
                    if b is not LAST or h + 2 < N:
                        exps(j0 + h + 2, (h + 2) % N)
                    if h == 11 and b is not LAST:
                        xnt_high(b + 1)
                    if h % 2 == 1 and (b is not LAST or h < 12):
                        act.wait_ge(v_ps, b * 8 + 3 + h // 2)
                        values_hi((2 + h // 2) % 8)
                    if h == 15 and b is LAST:
                        gate(0, 0, 0)
                    act.wait_ge(o_ps, j0 + h + 1)
                    nc.scalar.copy(att[h % 2][0][:, :], p_o[:, h % 2, :]).then_inc(o_hi, 1)
                    if b is LAST:
                        if h == 12:
                            xnt2_high(1, p_x0)
                        if h == 15:
                            tanh(0)
                            shared_gate(0)
                    for n in split_now(b, h):
                        split_hi(n)

            def gate(base, ubase, e):
                u = 0 if e == 0 else e + 2
                act.wait_ge(u_ps, ubase + u + 1)
                nc.scalar.activation(silu[:, e % 2, 0:I], p_u[u % 4][:, 0:I], ACT.Silu).then_inc(silu_done, 1)

            def shared_gate(ubase):
                act.wait_ge(u_ps, ubase + 2)
                nc.scalar.activation(silu[:, 2, :], p_u[1][:, 0:UW], ACT.Silu).then_inc(silu_done, 1)

            def tanh(tile):
                act.wait_ge(gap_done, tile + 1)
                nc.scalar.activation(th[:, :], gap[:, :], ACT.Tanh, scale=0.5).then_inc(th_done, 1)

            def acts_high(t, g):
                act.wait_ge(a_ps, t * NG + g + 1)
                for lo, hi, r in spans(g):
                    op = nc.scalar.copy(actt[g % 2][0][0:r, lo:hi, :], p_a[g % 2][0:r, lo:hi, :])
                op.then_inc(a_hi, 1)

            def xnt2_high(count, src=p_x):
                act.wait_ge(xnt2_ps, count)
                nc.scalar.copy(xnt2[0][:, :, :], src[:, 0:DC, :]).then_inc(xnt2_hi, 1)

            for n in range(4):
                split_hi(n)
            xnt_high(0)
            for n in range(4, 10):
                split_hi(n)
            act.wait_ge(rope_add, 1)
            qkt_high(0)
            act.wait_ge(v_ps, 1)
            values_hi(0)
            split_hi(10)
            act.wait_ge(rope_add, 2)
            qkt_high(1)
            split_hi(11)
            exps(0, 0)
            act.wait_ge(v_ps, 2)
            values_hi(1)
            act.wait_ge(inv_done, 1)
            normalise(0)
            act.wait_ge(rope_add, 3)
            act.wait_ge(s_ps, 1)
            qkt_high(2)
            exps(1, 1)
            sequence(FIRST)
            with act.Fori(1, LAST) as b:
                sequence(b)
            sequence(LAST)

            for n in plan["rest"]:
                split_hi(n)

            def tile_step(t):
                for e in range(1, E):
                    if e >= 2:
                        act.wait_ge(act_done, t * NR + (1 if e == 2 else e))
                    gate(t * NR, t * NU, e)
                    if e == 2:
                        acts_high(t, 0)
                    if e == 5:
                        acts_high(t, 1)
                more = t is not LAST_TILE
                if more:
                    xnt2_high(t + 2)
                acts_high(t, 2)
                if more:
                    act.wait_ge(act_done, t * NR + 8)
                    gate(t * NR + NR, t * NU + NU, 0)
                    tanh(t + 1)
                acts_high(t, 3)
                if more:
                    shared_gate(t * NU + NU)

            with act.Fori(0, LAST_TILE) as t:
                tile_step(t)
            tile_step(LAST_TILE)

        @block.gpsimd
        def _(pool):
            def rsqrt(ready_sem, step_sem, done_sem, count, n):
                pool.wait_ge(ready_sem, count)
                pool.nop(nofuse=True)
                nc.gpsimd.tensor_scalar(vare[:, 0:n], mv[:, 0:n, 1], EPS, 1.0, ALU.add, ALU.mult).then_inc(step_sem, 1)
                pool.wait_ge(step_sem, count)
                nc.gpsimd.tensor_tensor(rstd[:, 0:n], vare[:, 0:n], mhalf[:, 0:n], ALU.pow).then_inc(done_sem, 1)

            def low(h):
                a = h % 2
                nc.gpsimd.tensor_tensor(qkt[a][1][:, :, :], roped[:, a], qkt[a][0][:, :, :],
                                        ALU.subtract).then_inc(qkt_lo, 1)

            def sequence(b):
                j0 = b * N
                for h in range(N):
                    if b is not LAST or h + 3 < N:
                        pool.wait_ge(rope_mul, j0 + h + 4)
                        pool.wait_ge(s_ps, j0 + h + 2)
                        rope_sum(nc.gpsimd, (h + 3) % N)
                        pool.wait_ge(qkt_hi, j0 + h + 4)
                        low((h + 3) % N)
                    if h == 6 and b is not LAST:
                        rsqrt(mv_done, vare_done, rstd_done, b + 2, ST)
                    if h == 6 and b is LAST:
                        rsqrt(mv2_done, vare2_done, rstd2_done, 1, 1)
                    for n in split_now(b, h - 1):
                        if lo_by(n) == 1:
                            split_lo(n)
                for n in split_now(b, N - 1):
                    if lo_by(n) == 1:
                        split_lo(n)

            def split_lo(n):
                _, seen = pieces[n]
                pool.wait_ge(w_hi, n + 1)
                for view, hi, lo in seen:
                    op = nc.gpsimd.tensor_tensor(lo, view(stage[:, n % NSTAGE, :]), hi, ALU.subtract)
                op.then_inc(w_lo[1], 1)

            rsqrt(mv_done, vare_done, rstd_done, 1, ST)
            for n in (1, 3, 6, 8):
                split_lo(n)
            for h in range(3):
                if h > 0:
                    pool.wait_ge(rope_mul, h + 1)
                    if h == 2:
                        pool.wait_ge(s_ps, 1)
                    rope_sum(nc.gpsimd, h)
                pool.wait_ge(qkt_hi, h + 1)
                low(h)
                if h == 1:
                    split_lo(11)
            sequence(FIRST)
            with pool.Fori(1, LAST) as b:
                sequence(b)
            sequence(LAST)
            for n in plan["rest"]:
                if lo_by(n) == 1:
                    split_lo(n)
            with pool.Fori(0, LAST_TILE) as t:
                rsqrt(mv2_done, vare2_done, rstd2_done, t + 2, 1)


ready = [2 + max(0, -(-(min(g[-1] * P + P, AW) - SI - I) // I)) for g in GROUPS]


def read_by(u):
    return (1, 2, 2)[u] if u < 3 else u


def spans(g):
    n = len(GROUPS[g])
    return [(0, n, P)] if g < NG - 1 or TAIL == P else [(0, n - 1, P), (n - 1, n, TAIL)]


def shape_constants():
    fraction = (np.float32(2.0) * np.arange(H // 2, dtype=np.float32)) / np.float32(H)
    timescale = np.power(np.float32(10000.0), fraction, dtype=np.float32)
    angle = np.arange(S, dtype=np.float32)[None, :] / timescale[:, None]
    cos, sin = np.cos(angle).astype(np.float32), np.sin(angle).astype(np.float32)
    row, col = np.arange(P)[:, None], np.arange(P)[None, :]
    diagonal = np.where(col <= row, 0.0, MASKED)
    return {
        "cos_t": np.concatenate([cos, cos]),
        "sin_t": np.concatenate([-sin, sin]),
        "mask_t": np.concatenate([np.zeros((P, P)), diagonal], axis=1).astype(np.float32),
        "ident_t": np.eye(P, dtype=np.float32),
        "before_t": np.broadcast_to(np.tril(np.ones((E, E), np.float32), -1), (P, E, E)).copy(),
    }


_INS = ["L0_attn_x", "L0_attn_wq", "L0_attn_wk", "L0_attn_wv", "L0_attn_wo", "L0_ffn_gate_w", "L0_ffn_w1",
        "L0_ffn_w3", "L0_ffn_w2", "L0_ffn_sw1", "L0_ffn_sw3", "L0_ffn_sw2"]


def kernel(**inputs):
    import concourse.bacc as _bacc
    from concourse.bass_utils import run_bass_kernel_spmd as _run

    nc = _bacc.Bacc("TRN2", target_bir_lowering=False, num_devices=1)
    arrays, args = {}, []
    for name, a in [(n, inputs[n]) for n in _INS] + list(shape_constants().items()):
        a = np.ascontiguousarray(a)
        arrays[f"in_{name}"] = a
        args.append(nc.dram_tensor(f"in_{name}", a.shape, mybir.dt.from_np(a.dtype), kind="ExternalInput").ap())
    args.append(nc.dram_tensor("out_x", (B, S, D), F32, kind="ExternalOutput").ap())
    build(nc, *args)
    r = _run(nc, [arrays], core_ids=[0])
    return r.results[0]["out_x"]
```
